# Optimizing a Trainium2 kernel written in Bass

```python
import numpy as np
import jax
import jax.numpy as jnp

def _softmax(x, axis=-1):
    return jax.nn.softmax(x, axis=axis)

def _gelu(x):
    return jax.nn.gelu(x, approximate=True)

def _silu(x):
    return jax.nn.silu(x)

def _sigmoid(x):
    return jax.nn.sigmoid(x)

def _layernorm(x, axis=-1, eps=1e-05):
    m = jnp.mean(x, axis=axis, keepdims=True)
    v = jnp.var(x, axis=axis, keepdims=True)
    return (x - m) / jnp.sqrt(v + eps)

def _scatter_add(tgt, idx, src, axis=0):
    return tgt.at[idx].add(src)

def _segment_sum(src, seg, n):
    return jax.ops.segment_sum(src, seg, n)
kernel_name = 'mk_recurrent_d4_jaxref_r8_b26b24'

def setup_inputs(seed: int=0):
    np.random.seed(seed)
    _w = jnp.asarray

    def _L0_attn_setup():
        import jax, jax.numpy as jnp
        import numpy as np
        D_MODEL = 128
        EXPAND = 2
        D_INNER = D_MODEL * EXPAND
        D_STATE = 16
        DT_RANK = int(np.ceil(D_MODEL / 16))
        D_CONV = 4
        EPS = 1e-05
        BATCH, SEQLEN = (4, 256)

        def _reference_tuple_inner(x, norm_w, in_proj_w, conv_w, conv_b, x_proj_w, dt_proj_w, dt_proj_b, A_log, D, out_proj_w):
            B, L, _ = x.shape
            xn = x * jax.lax.rsqrt(jnp.mean(x * x, axis=-1, keepdims=True) + EPS) * norm_w
            u, res = jnp.split(xn @ in_proj_w, 2, axis=-1)
            u_pad = jnp.pad(u, ((0, 0), (D_CONV - 1, 0), (0, 0)))
            u = sum((conv_w[:, k] * u_pad[:, k:k + L, :] for k in range(D_CONV))) + conv_b
            u = jax.nn.silu(u)
            dbc = u @ x_proj_w
            dt, Bm, Cm = jnp.split(dbc, [DT_RANK, DT_RANK + D_STATE], axis=-1)
            delta = jax.nn.softplus(dt @ dt_proj_w + dt_proj_b)
            A = -jnp.exp(A_log)

            def step(h, inp):
                d_t, B_t, C_t, u_t = inp
                dA = jnp.exp(d_t[:, :, None] * A)
                dBu = (d_t * u_t)[:, :, None] * B_t[:, None, :]
                h = dA * h + dBu
                y = jnp.einsum('bds,bs->bd', h, C_t)
                return (h, y)
            h0 = jnp.zeros((B, D_INNER, D_STATE), u.dtype)
            seq = (jnp.swapaxes(delta, 0, 1), jnp.swapaxes(Bm, 0, 1), jnp.swapaxes(Cm, 0, 1), jnp.swapaxes(u, 0, 1))
            hidden, ys = jax.lax.scan(step, h0, seq)
            y = jnp.swapaxes(ys, 0, 1) + u * D
            y = y * jax.nn.silu(res)
            out = y @ out_proj_w
            return (out, hidden)
        key = jax.random.key(seed)
        ks = jax.random.split(key, 8)
        f32 = jnp.float32
        sc = lambda k, shape, s=0.02: jax.random.normal(k, shape, dtype=f32) * s
        x = jax.random.normal(ks[0], (BATCH, SEQLEN, D_MODEL), dtype=f32)
        norm_w = jnp.ones((D_MODEL,), f32)
        in_proj_w = sc(ks[1], (D_MODEL, 2 * D_INNER))
        conv_w = sc(ks[2], (D_INNER, D_CONV), 0.1)
        conv_b = jnp.zeros((D_INNER,), f32)
        x_proj_w = sc(ks[3], (D_INNER, DT_RANK + 2 * D_STATE))
        dt_proj_w = sc(ks[4], (DT_RANK, D_INNER), 0.1)
        dt_proj_b = jnp.full((D_INNER,), float(np.log(np.expm1(0.01))), f32)
        A_log = jnp.log(jnp.broadcast_to(jnp.arange(1, D_STATE + 1, dtype=f32), (D_INNER, D_STATE)))
        D = jnp.ones((D_INNER,), f32)
        out_proj_w = sc(ks[5], (D_INNER, D_MODEL))
        return {'x': x, 'norm_w': norm_w, 'in_proj_w': in_proj_w, 'conv_w': conv_w, 'conv_b': conv_b, 'x_proj_w': x_proj_w, 'dt_proj_w': dt_proj_w, 'dt_proj_b': dt_proj_b, 'A_log': A_log, 'D': D, 'out_proj_w': out_proj_w}
    _L0_attn_in = _L0_attn_setup()

    def _L0_ffn_setup():
        import jax, jax.numpy as jnp
        import numpy as np
        DIM = 128
        DEPTH = 6
        HEADS = 16
        DIM_HEAD = 64
        WINDOW = 32
        INNER = HEADS * DIM_HEAD
        DIM_INNER = int(DIM * 4 * 2 / 3)
        QK_SCALE = 8.0

        def shift_tokens(t):
            a, s = jnp.split(t, 2, -1)
            s = jnp.pad(s, ((0, 0), (1, 0), (0, 0)))[:, :-1]
            return jnp.concatenate([a, s], -1)

        def l2norm(t):
            return t / jnp.maximum(jnp.linalg.norm(t, axis=-1, keepdims=True), 1e-12)

        def rotate_half(x):
            x1, x2 = jnp.split(x, 2, -1)
            return jnp.concatenate([-x2, x1], -1)

        def rotary_tables(n):
            half = jnp.arange(0, DIM_HEAD, 2, dtype=jnp.float32)
            inv_freq = 1.0 / 10000.0 ** (half / DIM_HEAD)
            t = jnp.arange(n, dtype=jnp.float32)
            freqs = t[:, None] * inv_freq[None, :]
            freqs = jnp.concatenate([freqs, freqs], -1)
            base_scale = (half + 0.4 * DIM_HEAD) / (1.4 * DIM_HEAD)
            power = (t - n // 2) / (WINDOW // 2)
            scale = base_scale[None, :] ** power[:, None]
            scale = jnp.concatenate([scale, scale], -1)
            return (freqs, scale)

        def local_attention(q, k, v):
            b, h, n, d = q.shape
            w = WINDOW
            nw = n // w
            bq = q.reshape(b, h, nw, w, d)
            bk = k.reshape(b, h, nw, w, d)
            bv = v.reshape(b, h, nw, w, d)

            def look(t):
                p = jnp.pad(t, ((0, 0), (0, 0), (1, 0), (0, 0), (0, 0)))
                return jnp.concatenate([p[:, :, :nw], p[:, :, 1:]], axis=3)
            bk2, bv2 = (look(bk), look(bv))
            seq = jnp.arange(n).reshape(nw, w)
            seq_p = jnp.pad(seq, ((1, 0), (0, 0)), constant_values=-1)
            jt = jnp.concatenate([seq_p[:nw], seq_p[1:]], axis=1)
            it = seq[:, :, None]
            jb = jt[:, None, :]
            mask = (it < jb) | (it > jb + w) | (jb == -1)
            sim = jnp.einsum('bhwie,bhwje->bhwij', bq, bk2) * QK_SCALE
            sim = jnp.where(mask, -jnp.finfo(sim.dtype).max, sim)
            attn = jax.nn.softmax(sim, -1)
            out = jnp.einsum('bhwij,bhwje->bhwie', attn, bv2)
            return out.reshape(b, h, n, d)

        def attn_layer(x, Wqkv, qs, ksc, Wo):
            b, n, _ = x.shape
            qkv = x @ Wqkv
            q, k, v = jnp.split(qkv, 3, -1)
            sh = lambda t: t.reshape(b, n, HEADS, DIM_HEAD).transpose(0, 2, 1, 3)
            q, k, v = (sh(q), sh(k), sh(v))
            q = l2norm(q) * qs
            k = l2norm(k) * ksc
            freqs, scale = rotary_tables(n)
            cos, sin = (jnp.cos(freqs), jnp.sin(freqs))
            q = q * cos * scale + rotate_half(q) * sin * scale
            inv = 1.0 / scale
            k = k * cos * inv + rotate_half(k) * sin * inv
            out = local_attention(q, k, v)
            out = out.transpose(0, 2, 1, 3).reshape(b, n, INNER)
            return out @ Wo

        def ffn_layer(x, g, bln, W1, b1, W2, b2):
            mu = x.mean(-1, keepdims=True)
            var = ((x - mu) ** 2).mean(-1, keepdims=True)
            xn = (x - mu) / jnp.sqrt(var + 1e-05) * g + bln
            hg = xn @ W1 + b1
            a, gate = jnp.split(hg, 2, -1)
            return a * jax.nn.gelu(gate, approximate=False) @ W2 + b2
        key = jax.random.key(seed)
        ks = jax.random.split(key, 8)
        B, N = (2, 256)
        init = lambda k, shape: jax.random.normal(k, shape, jnp.float32) * 0.02
        return {'x': jax.random.normal(ks[0], (B, N, DIM), jnp.float32), 'Wqkv': init(ks[1], (DEPTH, DIM, 3 * INNER)), 'q_scale': jnp.ones((DEPTH, DIM_HEAD), jnp.float32), 'k_scale': jnp.ones((DEPTH, DIM_HEAD), jnp.float32), 'Wo': init(ks[2], (DEPTH, INNER, DIM)), 'ln_g': jnp.ones((DEPTH, DIM), jnp.float32), 'ln_b': jnp.zeros((DEPTH, DIM), jnp.float32), 'W1': init(ks[3], (DEPTH, DIM, 2 * DIM_INNER)), 'b1': jnp.zeros((DEPTH, 2 * DIM_INNER), jnp.float32), 'W2': init(ks[4], (DEPTH, DIM_INNER, DIM)), 'b2': jnp.zeros((DEPTH, DIM), jnp.float32)}
    _L0_ffn_in = _L0_ffn_setup()

    def _L1_attn_setup():
        import jax, jax.numpy as jnp
        import numpy as np
        B, L, DIM = (4, 512, 128)
        H, DQK, DV, DINNER, CHUNK = (16, 64, 64, 64, 64)
        BASE_LR, BASE_WD = (0.001, 0.9)
        key = jax.random.key(seed)
        ks = jax.random.split(key, 9)

        def s(k, shape, scale):
            return jax.random.normal(k, shape, jnp.float32) * scale
        return {'x': jax.random.normal(ks[0], (B, L, DIM), jnp.float32), 'Wq': s(ks[1], (H * DQK, DIM), DIM ** (-0.5)), 'Wk': s(ks[2], (H * DQK, DIM), DIM ** (-0.5)), 'Wv': s(ks[3], (H * DV, DIM), DIM ** (-0.5)), 'Wlr': s(ks[4], (2 * H, DIM), DIM ** (-0.5)), 'Wbeta': s(ks[5], (2 * H, DIM), DIM ** (-0.5)), 'Wo': s(ks[6], (DIM, H * DV), (H * DV) ** (-0.5)), 'W_in_init': s(ks[7], (1, DINNER, H, DQK), DQK ** (-0.5)), 'W_out_init': s(ks[8], (1, DINNER, H, DV), DINNER ** (-0.5))}
    _L1_attn_in = _L1_attn_setup()

    def _L1_ffn_setup():
        import jax, jax.numpy as jnp
        import numpy as np
        DIM = 128
        DEPTH = 2
        HEADS = 8
        DIM_HEAD = 64
        WINDOW = 64
        INNER = HEADS * DIM_HEAD
        HID = int(DIM * 4 * 2 / 3)
        B, N = (2, 1024)
        QK_SCALE = 8.0

        def shift_token(t):
            t1, t2 = jnp.split(t, 2, axis=-1)
            t2 = jnp.pad(t2, ((0, 0), (1, 0), (0, 0)))[:, :-1]
            return jnp.concatenate([t1, t2], axis=-1)

        def l2norm(t):
            return t / jnp.clip(jnp.linalg.norm(t, axis=-1, keepdims=True), 1e-12)

        def rotate_half(x):
            x1, x2 = jnp.split(x, 2, axis=-1)
            return jnp.concatenate([-x2, x1], axis=-1)

        def rotary_xpos(q, k):
            n = q.shape[-2]
            half_idx = jnp.arange(0, DIM_HEAD, 2, dtype=jnp.float32)
            inv_freq = 1.0 / 10000.0 ** (half_idx / DIM_HEAD)
            t = jnp.arange(n, dtype=jnp.float32)
            freqs = t[:, None] * inv_freq[None, :]
            freqs = jnp.concatenate([freqs, freqs], axis=-1)
            base = (half_idx + 0.4 * DIM_HEAD) / (1.4 * DIM_HEAD)
            power = (t - n // 2) / float(WINDOW // 2)
            scale = base[None, :] ** power[:, None]
            scale = jnp.concatenate([scale, scale], axis=-1)
            cos, sin = (jnp.cos(freqs), jnp.sin(freqs))
            q = q * cos * scale + rotate_half(q) * sin * scale
            k = k * cos / scale + rotate_half(k) * sin / scale
            return (q, k)

        def local_attention(q, k, v):
            b, h, n, d = q.shape
            w = n // WINDOW
            bq = q.reshape(b, h, w, WINDOW, d) * QK_SCALE
            bk = k.reshape(b, h, w, WINDOW, d)
            bv = v.reshape(b, h, w, WINDOW, d)

            def look_around(t):
                p = jnp.pad(t, ((0, 0), (0, 0), (1, 0), (0, 0), (0, 0)))
                return jnp.concatenate([p[:, :, :w], p[:, :, 1:]], axis=3)
            bk, bv = (look_around(bk), look_around(bv))
            bt = jnp.arange(n).reshape(w, WINDOW)
            btp = jnp.pad(bt, ((1, 0), (0, 0)), constant_values=-1)
            btk = jnp.concatenate([btp[:w], btp[1:]], axis=1)
            sim = jnp.einsum('bhwid,bhwjd->bhwij', bq, bk)
            i = bt[:, :, None]
            j = btk[:, None, :]
            mask = (i < j) | (i > j + WINDOW) | (j == -1)
            sim = jnp.where(mask, -jnp.finfo(sim.dtype).max, sim)
            attn = jax.nn.softmax(sim, axis=-1)
            out = jnp.einsum('bhwij,bhwjd->bhwid', attn, bv)
            return out.reshape(b, h, n, d)

        def _layer(x, wqkv, qs, ksc, wo, lg, lb, w1, b1, w2, b2):
            b, n, _ = x.shape
            h = shift_token(x)
            qkv = h @ wqkv
            q, k, v = jnp.split(qkv, 3, axis=-1)
            to_heads = lambda t: t.reshape(b, n, HEADS, DIM_HEAD).transpose(0, 2, 1, 3)
            q, k, v = (to_heads(q), to_heads(k), to_heads(v))
            q = l2norm(q) * qs
            k = l2norm(k) * ksc
            q, k = rotary_xpos(q, k)
            o = local_attention(q, k, v)
            o = o.transpose(0, 2, 1, 3).reshape(b, n, INNER)
            x = x + o @ wo
            h = shift_token(x)
            mu = h.mean(-1, keepdims=True)
            var = h.var(-1, keepdims=True)
            h = (h - mu) / jnp.sqrt(var + 1e-05) * lg + lb
            h = h @ w1 + b1
            a, g = jnp.split(h, 2, axis=-1)
            h = a * jax.nn.gelu(g, approximate=False)
            x = x + h @ w2 + b2
            return x
        key = jax.random.key(seed)
        ks = jax.random.split(key, 6)
        return {'x': jax.random.normal(ks[0], (B, N, DIM), jnp.float32), 'wqkv': jax.random.normal(ks[1], (DEPTH, DIM, 3 * INNER), jnp.float32) * 0.02, 'q_scale': jnp.ones((DEPTH, DIM_HEAD), jnp.float32), 'k_scale': jnp.ones((DEPTH, DIM_HEAD), jnp.float32), 'wo': jax.random.normal(ks[2], (DEPTH, INNER, DIM), jnp.float32) * 0.02, 'ln_g': jnp.ones((DEPTH, DIM), jnp.float32), 'ln_b': jnp.zeros((DEPTH, DIM), jnp.float32), 'w1': jax.random.normal(ks[3], (DEPTH, DIM, 2 * HID), jnp.float32) * 0.02, 'b1': jnp.zeros((DEPTH, 2 * HID), jnp.float32), 'w2': jax.random.normal(ks[4], (DEPTH, HID, DIM), jnp.float32) * 0.02, 'b2': jnp.zeros((DEPTH, DIM), jnp.float32)}
    _L1_ffn_in = _L1_ffn_setup()

    def _L2_attn_setup():
        import jax, jax.numpy as jnp
        import numpy as np
        BATCH, SEQ, D_MODEL = (4, 256, 128)
        D_INNER, D_STATE, D_CONV, DT_RANK = (2 * D_MODEL, 16, 4, D_MODEL // 16)
        LN_EPS = 1e-05

        def _mamba_core(xn, W_in, conv_w, conv_b, W_x, W_dt, b_dt, A_log, D_skip, W_out):
            b, l, _ = xn.shape
            xz = xn @ W_in
            xi, z = jnp.split(xz, 2, axis=-1)
            xp = jnp.pad(xi, ((0, 0), (D_CONV - 1, 0), (0, 0)))
            xc = sum((xp[:, k:k + l, :] * conv_w[:, k] for k in range(D_CONV))) + conv_b
            xc = jax.nn.silu(xc)
            dbl = xc @ W_x
            dt, Bm, Cm = jnp.split(dbl, [DT_RANK, DT_RANK + D_STATE], axis=-1)
            dt = jax.nn.softplus(dt @ W_dt + b_dt)
            A = -jnp.exp(A_log)

            def step(h, inputs):
                dt_t, B_t, C_t, x_t = inputs
                h = jnp.exp(dt_t[..., None] * A) * h + (dt_t * x_t)[..., None] * B_t[:, None, :]
                y = jnp.einsum('bdn,bn->bd', h, C_t)
                return (h, y)
            h0 = jnp.zeros((b, D_INNER, D_STATE), xc.dtype)
            _, ys = jax.lax.scan(step, h0, (dt.transpose(1, 0, 2), Bm.transpose(1, 0, 2), Cm.transpose(1, 0, 2), xc.transpose(1, 0, 2)))
            y = ys.transpose(1, 0, 2) + D_skip * xc
            y = y * jax.nn.silu(z)
            return y @ W_out
        key = jax.random.key(seed)
        ks = jax.random.split(key, 10)
        s = lambda fan: 1.0 / np.sqrt(fan)
        inp = {'x': jax.random.normal(ks[0], (BATCH, SEQ, D_MODEL), jnp.float32), 'gamma': jnp.ones((D_MODEL,), jnp.float32), 'beta': jnp.zeros((D_MODEL,), jnp.float32), 'W_in': jax.random.normal(ks[1], (D_MODEL, 2 * D_INNER), jnp.float32) * s(D_MODEL), 'conv_w': jax.random.normal(ks[2], (D_INNER, D_CONV), jnp.float32) * s(D_CONV), 'conv_b': jnp.zeros((D_INNER,), jnp.float32), 'W_x': jax.random.normal(ks[3], (D_INNER, DT_RANK + 2 * D_STATE), jnp.float32) * s(D_INNER), 'W_dt': jax.random.normal(ks[4], (DT_RANK, D_INNER), jnp.float32) * s(DT_RANK), 'b_dt': jax.random.uniform(ks[5], (D_INNER,), jnp.float32, -4.0, -2.0), 'A_log': jnp.broadcast_to(jnp.log(jnp.arange(1, D_STATE + 1, dtype=jnp.float32)), (D_INNER, D_STATE)).copy(), 'D_skip': jnp.ones((D_INNER,), jnp.float32), 'W_out': jax.random.normal(ks[6], (D_INNER, D_MODEL), jnp.float32) * s(D_INNER)}
        return inp
    _L2_attn_in = _L2_attn_setup()

    def _L2_ffn_setup():
        import jax, jax.numpy as jnp
        import numpy as np
        B, S, H = (2, 64, 128)
        E, I = (64, 64)
        K = 8
        G, TG = (8, 4)
        SCALE = 2.5
        T = B * S
        CAP = 64

        def _moe_forward(x, router_w, gate_w, up_w, down_w, shared_gate_w, shared_up_w, shared_down_w):
            b, s, h = x.shape
            tokens = x.reshape(-1, h)
            t = tokens.shape[0]
            logits = tokens @ router_w
            scores = jax.nn.sigmoid(logits)
            eg = E // G
            group_scores = scores.reshape(t, G, eg).max(axis=-1)
            _, sel_groups = jax.lax.top_k(group_scores, TG)
            group_mask = jnp.zeros((t, G), bool).at[jnp.arange(t)[:, None], sel_groups].set(True)
            expert_mask = jnp.repeat(group_mask, eg, axis=1)
            masked_scores = jnp.where(expert_mask, scores, 0.0)
            topk_w, topk_idx = jax.lax.top_k(masked_scores, K)
            topk_w = topk_w / jnp.clip(topk_w.sum(-1, keepdims=True), 1e-09)
            topk_w = topk_w * SCALE
            flat_e = topk_idx.reshape(-1)
            onehot = jax.nn.one_hot(flat_e, E, dtype=jnp.int32)
            prior = jnp.cumsum(onehot, axis=0) - onehot
            pos = jnp.take_along_axis(prior, flat_e[:, None], axis=1)[:, 0]
            valid = (pos < CAP).astype(tokens.dtype)
            pos_c = jnp.minimum(pos, CAP - 1)
            tidx = jnp.repeat(jnp.arange(t), K)
            dispatch = jnp.zeros((E, CAP, h), tokens.dtype)
            dispatch = dispatch.at[flat_e, pos_c].add(tokens[tidx] * valid[:, None])
            g = jnp.einsum('ech,ehi->eci', dispatch, gate_w)
            u = jnp.einsum('ech,ehi->eci', dispatch, up_w)
            expert_out = jnp.einsum('eci,eih->ech', jax.nn.silu(g) * u, down_w)
            gathered = expert_out[flat_e, pos_c]
            contrib = gathered * (topk_w.reshape(-1) * valid)[:, None]
            output = jnp.zeros((t, h), tokens.dtype).at[tidx].add(contrib)
            sg = jax.nn.silu(tokens @ shared_gate_w) * (tokens @ shared_up_w)
            output = output + sg @ shared_down_w
            return output.reshape(b, s, h)
        key = jax.random.key(seed)
        ks = jax.random.split(key, 9)
        s_h = 1.0 / np.sqrt(H)
        s_i = 1.0 / np.sqrt(I)
        return {'x': jax.random.normal(ks[0], (B, S, H), jnp.float32), 'router_w': jax.random.normal(ks[1], (H, E), jnp.float32) * s_h, 'gate_w': jax.random.normal(ks[2], (E, H, I), jnp.float32) * s_h, 'up_w': jax.random.normal(ks[3], (E, H, I), jnp.float32) * s_h, 'down_w': jax.random.normal(ks[4], (E, I, H), jnp.float32) * s_i, 'shared_gate_w': jax.random.normal(ks[5], (H, I), jnp.float32) * s_h, 'shared_up_w': jax.random.normal(ks[6], (H, I), jnp.float32) * s_h, 'shared_down_w': jax.random.normal(ks[7], (I, H), jnp.float32) * s_i}
    _L2_ffn_in = _L2_ffn_setup()

    def _L3_attn_setup():
        import jax, jax.numpy as jnp
        import numpy as np
        DIM = 128
        N_QUAT = DIM // 4
        LN_EPS = 1e-05
        NORM_EPS = 1e-12

        def quat_mul(q1, q2):
            r1, i1, j1, k1 = (q1[..., 0], q1[..., 1], q1[..., 2], q1[..., 3])
            r2, i2, j2, k2 = (q2[..., 0], q2[..., 1], q2[..., 2], q2[..., 3])
            r = r1 * r2 - i1 * i2 - j1 * j2 - k1 * k2
            i = r1 * i2 + i1 * r2 + j1 * k2 - k1 * j2
            j = r1 * j2 - i1 * k2 + j1 * r2 + k1 * i2
            k = r1 * k2 + i1 * j2 - j1 * i2 + k1 * r2
            return jnp.stack([r, i, j, k], axis=-1)

        def quat_conj(q):
            return q * jnp.array([1.0, -1.0, -1.0, -1.0], dtype=q.dtype)
        key = jax.random.key(seed)
        ks = jax.random.split(key, 7)
        B, L, D = (4, 512, DIM)
        s = 1.0 / np.sqrt(D)
        return {'x': jax.random.normal(ks[0], (B, L, D), dtype=jnp.float32), 'Wk': jax.random.normal(ks[1], (D, D), dtype=jnp.float32) * s, 'bk': jnp.zeros((D,), dtype=jnp.float32), 'Wv': jax.random.normal(ks[2], (D, D), dtype=jnp.float32) * s, 'bv': jnp.zeros((D,), dtype=jnp.float32), 'ln_g': jnp.ones((D,), dtype=jnp.float32), 'ln_b': jnp.zeros((D,), dtype=jnp.float32), 'Wo': jax.random.normal(ks[3], (D, D), dtype=jnp.float32) * s, 'bo': jnp.zeros((D,), dtype=jnp.float32)}
    _L3_attn_in = _L3_attn_setup()

    def _L3_ffn_setup():
        import jax, jax.numpy as jnp
        import numpy as np
        B, S, H = (4, 256, 128)
        E = 8
        GS = 2
        NG = E // GS
        F = int(H * 4 * (2.0 / 3.0))
        key = jax.random.key(seed)
        ks = jax.random.split(key, 7)
        sc_h = 1.0 / np.sqrt(H)
        sc_f = 1.0 / np.sqrt(F)
        return {'x': jax.random.normal(ks[0], (B, S, H), dtype=jnp.float32), 'Wr': jax.random.normal(ks[1], (H, E), dtype=jnp.float32) * sc_h, 'br': jnp.zeros((E,), dtype=jnp.float32), 'W_up': jax.random.normal(ks[2], (NG, H, F), dtype=jnp.float32) * sc_h, 'b_up': jax.random.normal(ks[3], (NG, F), dtype=jnp.float32) * 0.01, 'W_down': jax.random.normal(ks[4], (E, F, H), dtype=jnp.float32) * sc_f, 'b_down': jax.random.normal(ks[5], (E, H), dtype=jnp.float32) * 0.01}
    _L3_ffn_in = _L3_ffn_setup()
    _d = {'L0_attn_x': _L0_attn_in['x'], 'L0_attn_norm_w': _L0_attn_in['norm_w'], 'L0_attn_in_proj_w': _L0_attn_in['in_proj_w'], 'L0_attn_conv_w': _L0_attn_in['conv_w'], 'L0_attn_conv_b': _L0_attn_in['conv_b'], 'L0_attn_x_proj_w': _L0_attn_in['x_proj_w'], 'L0_attn_dt_proj_w': _L0_attn_in['dt_proj_w'], 'L0_attn_dt_proj_b': _L0_attn_in['dt_proj_b'], 'L0_attn_A_log': _L0_attn_in['A_log'], 'L0_attn_D': _L0_attn_in['D'], 'L0_attn_out_proj_w': _L0_attn_in['out_proj_w'], 'L0_ffn_Wqkv': _L0_ffn_in['Wqkv'], 'L0_ffn_q_scale': _L0_ffn_in['q_scale'], 'L0_ffn_k_scale': _L0_ffn_in['k_scale'], 'L0_ffn_Wo': _L0_ffn_in['Wo'], 'L0_ffn_ln_g': _L0_ffn_in['ln_g'], 'L0_ffn_ln_b': _L0_ffn_in['ln_b'], 'L0_ffn_W1': _L0_ffn_in['W1'], 'L0_ffn_b1': _L0_ffn_in['b1'], 'L0_ffn_W2': _L0_ffn_in['W2'], 'L0_ffn_b2': _L0_ffn_in['b2'], 'L1_attn_Wq': _L1_attn_in['Wq'], 'L1_attn_Wk': _L1_attn_in['Wk'], 'L1_attn_Wv': _L1_attn_in['Wv'], 'L1_attn_Wlr': _L1_attn_in['Wlr'], 'L1_attn_Wbeta': _L1_attn_in['Wbeta'], 'L1_attn_Wo': _L1_attn_in['Wo'], 'L1_attn_W_in_init': _L1_attn_in['W_in_init'], 'L1_attn_W_out_init': _L1_attn_in['W_out_init'], 'L1_ffn_wqkv': _L1_ffn_in['wqkv'], 'L1_ffn_q_scale': _L1_ffn_in['q_scale'], 'L1_ffn_k_scale': _L1_ffn_in['k_scale'], 'L1_ffn_wo': _L1_ffn_in['wo'], 'L1_ffn_ln_g': _L1_ffn_in['ln_g'], 'L1_ffn_ln_b': _L1_ffn_in['ln_b'], 'L1_ffn_w1': _L1_ffn_in['w1'], 'L1_ffn_b1': _L1_ffn_in['b1'], 'L1_ffn_w2': _L1_ffn_in['w2'], 'L1_ffn_b2': _L1_ffn_in['b2'], 'L2_attn_gamma': _L2_attn_in['gamma'], 'L2_attn_beta': _L2_attn_in['beta'], 'L2_attn_W_in': _L2_attn_in['W_in'], 'L2_attn_conv_w': _L2_attn_in['conv_w'], 'L2_attn_conv_b': _L2_attn_in['conv_b'], 'L2_attn_W_x': _L2_attn_in['W_x'], 'L2_attn_W_dt': _L2_attn_in['W_dt'], 'L2_attn_b_dt': _L2_attn_in['b_dt'], 'L2_attn_A_log': _L2_attn_in['A_log'], 'L2_attn_D_skip': _L2_attn_in['D_skip'], 'L2_attn_W_out': _L2_attn_in['W_out'], 'L2_ffn_router_w': _L2_ffn_in['router_w'], 'L2_ffn_gate_w': _L2_ffn_in['gate_w'], 'L2_ffn_up_w': _L2_ffn_in['up_w'], 'L2_ffn_down_w': _L2_ffn_in['down_w'], 'L2_ffn_shared_gate_w': _L2_ffn_in['shared_gate_w'], 'L2_ffn_shared_up_w': _L2_ffn_in['shared_up_w'], 'L2_ffn_shared_down_w': _L2_ffn_in['shared_down_w'], 'L3_attn_Wk': _L3_attn_in['Wk'], 'L3_attn_bk': _L3_attn_in['bk'], 'L3_attn_Wv': _L3_attn_in['Wv'], 'L3_attn_bv': _L3_attn_in['bv'], 'L3_attn_ln_g': _L3_attn_in['ln_g'], 'L3_attn_ln_b': _L3_attn_in['ln_b'], 'L3_attn_Wo': _L3_attn_in['Wo'], 'L3_attn_bo': _L3_attn_in['bo'], 'L3_ffn_Wr': _L3_ffn_in['Wr'], 'L3_ffn_br': _L3_ffn_in['br'], 'L3_ffn_W_up': _L3_ffn_in['W_up'], 'L3_ffn_b_up': _L3_ffn_in['b_up'], 'L3_ffn_W_down': _L3_ffn_in['W_down'], 'L3_ffn_b_down': _L3_ffn_in['b_down']}
    _x0 = _d['L0_attn_x']
    _d['L0_attn_x'] = jax.random.normal(jax.random.fold_in(jax.random.key(seed), 1), (8, 512, 128), dtype=_x0.dtype)
    del _x0
    return _d

def reference(L0_attn_x, L0_attn_norm_w, L0_attn_in_proj_w, L0_attn_conv_w, L0_attn_conv_b, L0_attn_x_proj_w, L0_attn_dt_proj_w, L0_attn_dt_proj_b, L0_attn_A_log, L0_attn_D, L0_attn_out_proj_w, L0_ffn_Wqkv, L0_ffn_q_scale, L0_ffn_k_scale, L0_ffn_Wo, L0_ffn_ln_g, L0_ffn_ln_b, L0_ffn_W1, L0_ffn_b1, L0_ffn_W2, L0_ffn_b2, L1_attn_Wq, L1_attn_Wk, L1_attn_Wv, L1_attn_Wlr, L1_attn_Wbeta, L1_attn_Wo, L1_attn_W_in_init, L1_attn_W_out_init, L1_ffn_wqkv, L1_ffn_q_scale, L1_ffn_k_scale, L1_ffn_wo, L1_ffn_ln_g, L1_ffn_ln_b, L1_ffn_w1, L1_ffn_b1, L1_ffn_w2, L1_ffn_b2, L2_attn_gamma, L2_attn_beta, L2_attn_W_in, L2_attn_conv_w, L2_attn_conv_b, L2_attn_W_x, L2_attn_W_dt, L2_attn_b_dt, L2_attn_A_log, L2_attn_D_skip, L2_attn_W_out, L2_ffn_router_w, L2_ffn_gate_w, L2_ffn_up_w, L2_ffn_down_w, L2_ffn_shared_gate_w, L2_ffn_shared_up_w, L2_ffn_shared_down_w, L3_attn_Wk, L3_attn_bk, L3_attn_Wv, L3_attn_bv, L3_attn_ln_g, L3_attn_ln_b, L3_attn_Wo, L3_attn_bo, L3_ffn_Wr, L3_ffn_br, L3_ffn_W_up, L3_ffn_b_up, L3_ffn_W_down, L3_ffn_b_down):

    def _L0_attn_ref(x, norm_w, in_proj_w, conv_w, conv_b, x_proj_w, dt_proj_w, dt_proj_b, A_log, D, out_proj_w):
        import jax, jax.numpy as jnp
        import numpy as np
        D_MODEL = 128
        EXPAND = 2
        D_INNER = D_MODEL * EXPAND
        D_STATE = 16
        DT_RANK = int(np.ceil(D_MODEL / 16))
        D_CONV = 4
        EPS = 1e-05
        BATCH, SEQLEN = (4, 256)

        def _reference_tuple_inner(x, norm_w, in_proj_w, conv_w, conv_b, x_proj_w, dt_proj_w, dt_proj_b, A_log, D, out_proj_w):
            B, L, _ = x.shape
            xn = x * jax.lax.rsqrt(jnp.mean(x * x, axis=-1, keepdims=True) + EPS) * norm_w
            u, res = jnp.split(xn @ in_proj_w, 2, axis=-1)
            u_pad = jnp.pad(u, ((0, 0), (D_CONV - 1, 0), (0, 0)))
            u = sum((conv_w[:, k] * u_pad[:, k:k + L, :] for k in range(D_CONV))) + conv_b
            u = jax.nn.silu(u)
            dbc = u @ x_proj_w
            dt, Bm, Cm = jnp.split(dbc, [DT_RANK, DT_RANK + D_STATE], axis=-1)
            delta = jax.nn.softplus(dt @ dt_proj_w + dt_proj_b)
            A = -jnp.exp(A_log)

            def step(h, inp):
                d_t, B_t, C_t, u_t = inp
                dA = jnp.exp(d_t[:, :, None] * A)
                dBu = (d_t * u_t)[:, :, None] * B_t[:, None, :]
                h = dA * h + dBu
                y = jnp.einsum('bds,bs->bd', h, C_t)
                return (h, y)
            h0 = jnp.zeros((B, D_INNER, D_STATE), u.dtype)
            seq = (jnp.swapaxes(delta, 0, 1), jnp.swapaxes(Bm, 0, 1), jnp.swapaxes(Cm, 0, 1), jnp.swapaxes(u, 0, 1))
            hidden, ys = jax.lax.scan(step, h0, seq)
            y = jnp.swapaxes(ys, 0, 1) + u * D
            y = y * jax.nn.silu(res)
            out = y @ out_proj_w
            return (out, hidden)
        return _reference_tuple_inner(x, norm_w, in_proj_w, conv_w, conv_b, x_proj_w, dt_proj_w, dt_proj_b, A_log, D, out_proj_w)[0]

    def _L0_ffn_ref(x, Wqkv, q_scale, k_scale, Wo, ln_g, ln_b, W1, b1, W2, b2):
        import jax, jax.numpy as jnp
        import numpy as np
        DIM = 128
        DEPTH = 6
        HEADS = 16
        DIM_HEAD = 64
        WINDOW = 32
        INNER = HEADS * DIM_HEAD
        DIM_INNER = int(DIM * 4 * 2 / 3)
        QK_SCALE = 8.0

        def shift_tokens(t):
            a, s = jnp.split(t, 2, -1)
            s = jnp.pad(s, ((0, 0), (1, 0), (0, 0)))[:, :-1]
            return jnp.concatenate([a, s], -1)

        def l2norm(t):
            return t / jnp.maximum(jnp.linalg.norm(t, axis=-1, keepdims=True), 1e-12)

        def rotate_half(x):
            x1, x2 = jnp.split(x, 2, -1)
            return jnp.concatenate([-x2, x1], -1)

        def rotary_tables(n):
            half = jnp.arange(0, DIM_HEAD, 2, dtype=jnp.float32)
            inv_freq = 1.0 / 10000.0 ** (half / DIM_HEAD)
            t = jnp.arange(n, dtype=jnp.float32)
            freqs = t[:, None] * inv_freq[None, :]
            freqs = jnp.concatenate([freqs, freqs], -1)
            base_scale = (half + 0.4 * DIM_HEAD) / (1.4 * DIM_HEAD)
            power = (t - n // 2) / (WINDOW // 2)
            scale = base_scale[None, :] ** power[:, None]
            scale = jnp.concatenate([scale, scale], -1)
            return (freqs, scale)

        def local_attention(q, k, v):
            b, h, n, d = q.shape
            w = WINDOW
            nw = n // w
            bq = q.reshape(b, h, nw, w, d)
            bk = k.reshape(b, h, nw, w, d)
            bv = v.reshape(b, h, nw, w, d)

            def look(t):
                p = jnp.pad(t, ((0, 0), (0, 0), (1, 0), (0, 0), (0, 0)))
                return jnp.concatenate([p[:, :, :nw], p[:, :, 1:]], axis=3)
            bk2, bv2 = (look(bk), look(bv))
            seq = jnp.arange(n).reshape(nw, w)
            seq_p = jnp.pad(seq, ((1, 0), (0, 0)), constant_values=-1)
            jt = jnp.concatenate([seq_p[:nw], seq_p[1:]], axis=1)
            it = seq[:, :, None]
            jb = jt[:, None, :]
            mask = (it < jb) | (it > jb + w) | (jb == -1)
            sim = jnp.einsum('bhwie,bhwje->bhwij', bq, bk2) * QK_SCALE
            sim = jnp.where(mask, -jnp.finfo(sim.dtype).max, sim)
            attn = jax.nn.softmax(sim, -1)
            out = jnp.einsum('bhwij,bhwje->bhwie', attn, bv2)
            return out.reshape(b, h, n, d)

        def attn_layer(x, Wqkv, qs, ksc, Wo):
            b, n, _ = x.shape
            qkv = x @ Wqkv
            q, k, v = jnp.split(qkv, 3, -1)
            sh = lambda t: t.reshape(b, n, HEADS, DIM_HEAD).transpose(0, 2, 1, 3)
            q, k, v = (sh(q), sh(k), sh(v))
            q = l2norm(q) * qs
            k = l2norm(k) * ksc
            freqs, scale = rotary_tables(n)
            cos, sin = (jnp.cos(freqs), jnp.sin(freqs))
            q = q * cos * scale + rotate_half(q) * sin * scale
            inv = 1.0 / scale
            k = k * cos * inv + rotate_half(k) * sin * inv
            out = local_attention(q, k, v)
            out = out.transpose(0, 2, 1, 3).reshape(b, n, INNER)
            return out @ Wo

        def ffn_layer(x, g, bln, W1, b1, W2, b2):
            mu = x.mean(-1, keepdims=True)
            var = ((x - mu) ** 2).mean(-1, keepdims=True)
            xn = (x - mu) / jnp.sqrt(var + 1e-05) * g + bln
            hg = xn @ W1 + b1
            a, gate = jnp.split(hg, 2, -1)
            return a * jax.nn.gelu(gate, approximate=False) @ W2 + b2
        for i in range(DEPTH):
            x = attn_layer(shift_tokens(x), Wqkv[i], q_scale[i], k_scale[i], Wo[i]) + x
            x = ffn_layer(shift_tokens(x), ln_g[i], ln_b[i], W1[i], b1[i], W2[i], b2[i]) + x
        return x

    def _L1_attn_ref(x, Wq, Wk, Wv, Wlr, Wbeta, Wo, W_in_init, W_out_init):
        import jax, jax.numpy as jnp
        import numpy as np
        B, L, DIM = (4, 512, 128)
        H, DQK, DV, DINNER, CHUNK = (16, 64, 64, 64, 64)
        BASE_LR, BASE_WD = (0.001, 0.9)
        b, l, _ = x.shape
        nc = l // CHUNK
        q = jax.nn.silu(x @ Wq.T).reshape(b, l, H, DQK)
        k = jax.nn.silu(x @ Wk.T).reshape(b, l, H, DQK)
        v = (x @ Wv.T).reshape(b, l, H, DV)
        lr = jax.nn.sigmoid(x @ Wlr.T) * BASE_LR
        wd = jax.nn.sigmoid(x @ Wbeta.T) * BASE_WD

        def chunked(t):
            return jnp.moveaxis(t.reshape(b, nc, CHUNK, *t.shape[2:]), 1, 0)
        qc, kc, vc = (chunked(q), chunked(k), chunked(v))
        lr_c = chunked(lr).mean(axis=2)
        wd_c = chunked(wd).mean(axis=2)
        lr_in, lr_out = (lr_c[..., :H], lr_c[..., H:])
        wd_in, wd_out = (wd_c[..., :H], wd_c[..., H:])
        W_in0 = jnp.broadcast_to(W_in_init, (b, DINNER, H, DQK))
        W_out0 = jnp.broadcast_to(W_out_init, (b, DINNER, H, DV))

        def step(carry, xs):
            W_in, W_out = carry
            qi, ki, vi, li, lo, wi, wo = xs
            p_q = jax.nn.softmax(jnp.einsum('bnhd,bDhd->bnhD', qi, W_in), axis=1)
            o = jnp.einsum('bnhD,bDhd->bnhd', p_q, W_out)
            p = jax.nn.softmax(jnp.einsum('bnhd,bDhd->bnhD', ki, W_in), axis=1)
            grad_out = jnp.einsum('bnhD,bnhd->bDhd', -p, vi)
            a = jnp.einsum('bDhd,bnhd->bnhD', W_out, vi)
            s = jnp.sum(p * a, axis=-1, keepdims=True)
            g_z = -(p * a - p * s)
            grad_in = jnp.einsum('bnhd,bnhD->bDhd', ki, g_z)
            W_in = wi[:, None, :, None] * W_in - li[:, None, :, None] * grad_in
            W_out = wo[:, None, :, None] * W_out - lo[:, None, :, None] * grad_out
            return ((W_in, W_out), o)
        _, outs = jax.lax.scan(step, (W_in0, W_out0), (qc, kc, vc, lr_in, lr_out, wd_in, wd_out))
        o = jnp.moveaxis(outs, 0, 1).reshape(b, l, H * DV)
        return o @ Wo.T

    def _L1_ffn_ref(x, wqkv, q_scale, k_scale, wo, ln_g, ln_b, w1, b1, w2, b2):
        import jax, jax.numpy as jnp
        import numpy as np
        DIM = 128
        DEPTH = 2
        HEADS = 8
        DIM_HEAD = 64
        WINDOW = 64
        INNER = HEADS * DIM_HEAD
        HID = int(DIM * 4 * 2 / 3)
        B, N = (2, 1024)
        QK_SCALE = 8.0

        def shift_token(t):
            t1, t2 = jnp.split(t, 2, axis=-1)
            t2 = jnp.pad(t2, ((0, 0), (1, 0), (0, 0)))[:, :-1]
            return jnp.concatenate([t1, t2], axis=-1)

        def l2norm(t):
            return t / jnp.clip(jnp.linalg.norm(t, axis=-1, keepdims=True), 1e-12)

        def rotate_half(x):
            x1, x2 = jnp.split(x, 2, axis=-1)
            return jnp.concatenate([-x2, x1], axis=-1)

        def rotary_xpos(q, k):
            n = q.shape[-2]
            half_idx = jnp.arange(0, DIM_HEAD, 2, dtype=jnp.float32)
            inv_freq = 1.0 / 10000.0 ** (half_idx / DIM_HEAD)
            t = jnp.arange(n, dtype=jnp.float32)
            freqs = t[:, None] * inv_freq[None, :]
            freqs = jnp.concatenate([freqs, freqs], axis=-1)
            base = (half_idx + 0.4 * DIM_HEAD) / (1.4 * DIM_HEAD)
            power = (t - n // 2) / float(WINDOW // 2)
            scale = base[None, :] ** power[:, None]
            scale = jnp.concatenate([scale, scale], axis=-1)
            cos, sin = (jnp.cos(freqs), jnp.sin(freqs))
            q = q * cos * scale + rotate_half(q) * sin * scale
            k = k * cos / scale + rotate_half(k) * sin / scale
            return (q, k)

        def local_attention(q, k, v):
            b, h, n, d = q.shape
            w = n // WINDOW
            bq = q.reshape(b, h, w, WINDOW, d) * QK_SCALE
            bk = k.reshape(b, h, w, WINDOW, d)
            bv = v.reshape(b, h, w, WINDOW, d)

            def look_around(t):
                p = jnp.pad(t, ((0, 0), (0, 0), (1, 0), (0, 0), (0, 0)))
                return jnp.concatenate([p[:, :, :w], p[:, :, 1:]], axis=3)
            bk, bv = (look_around(bk), look_around(bv))
            bt = jnp.arange(n).reshape(w, WINDOW)
            btp = jnp.pad(bt, ((1, 0), (0, 0)), constant_values=-1)
            btk = jnp.concatenate([btp[:w], btp[1:]], axis=1)
            sim = jnp.einsum('bhwid,bhwjd->bhwij', bq, bk)
            i = bt[:, :, None]
            j = btk[:, None, :]
            mask = (i < j) | (i > j + WINDOW) | (j == -1)
            sim = jnp.where(mask, -jnp.finfo(sim.dtype).max, sim)
            attn = jax.nn.softmax(sim, axis=-1)
            out = jnp.einsum('bhwij,bhwjd->bhwid', attn, bv)
            return out.reshape(b, h, n, d)

        def _layer(x, wqkv, qs, ksc, wo, lg, lb, w1, b1, w2, b2):
            b, n, _ = x.shape
            h = shift_token(x)
            qkv = h @ wqkv
            q, k, v = jnp.split(qkv, 3, axis=-1)
            to_heads = lambda t: t.reshape(b, n, HEADS, DIM_HEAD).transpose(0, 2, 1, 3)
            q, k, v = (to_heads(q), to_heads(k), to_heads(v))
            q = l2norm(q) * qs
            k = l2norm(k) * ksc
            q, k = rotary_xpos(q, k)
            o = local_attention(q, k, v)
            o = o.transpose(0, 2, 1, 3).reshape(b, n, INNER)
            x = x + o @ wo
            h = shift_token(x)
            mu = h.mean(-1, keepdims=True)
            var = h.var(-1, keepdims=True)
            h = (h - mu) / jnp.sqrt(var + 1e-05) * lg + lb
            h = h @ w1 + b1
            a, g = jnp.split(h, 2, axis=-1)
            h = a * jax.nn.gelu(g, approximate=False)
            x = x + h @ w2 + b2
            return x
        for l in range(DEPTH):
            x = _layer(x, wqkv[l], q_scale[l], k_scale[l], wo[l], ln_g[l], ln_b[l], w1[l], b1[l], w2[l], b2[l])
        return x

    def _L2_attn_ref(x, gamma, beta, W_in, conv_w, conv_b, W_x, W_dt, b_dt, A_log, D_skip, W_out):
        import jax, jax.numpy as jnp
        import numpy as np
        BATCH, SEQ, D_MODEL = (4, 256, 128)
        D_INNER, D_STATE, D_CONV, DT_RANK = (2 * D_MODEL, 16, 4, D_MODEL // 16)
        LN_EPS = 1e-05

        def _mamba_core(xn, W_in, conv_w, conv_b, W_x, W_dt, b_dt, A_log, D_skip, W_out):
            b, l, _ = xn.shape
            xz = xn @ W_in
            xi, z = jnp.split(xz, 2, axis=-1)
            xp = jnp.pad(xi, ((0, 0), (D_CONV - 1, 0), (0, 0)))
            xc = sum((xp[:, k:k + l, :] * conv_w[:, k] for k in range(D_CONV))) + conv_b
            xc = jax.nn.silu(xc)
            dbl = xc @ W_x
            dt, Bm, Cm = jnp.split(dbl, [DT_RANK, DT_RANK + D_STATE], axis=-1)
            dt = jax.nn.softplus(dt @ W_dt + b_dt)
            A = -jnp.exp(A_log)

            def step(h, inputs):
                dt_t, B_t, C_t, x_t = inputs
                h = jnp.exp(dt_t[..., None] * A) * h + (dt_t * x_t)[..., None] * B_t[:, None, :]
                y = jnp.einsum('bdn,bn->bd', h, C_t)
                return (h, y)
            h0 = jnp.zeros((b, D_INNER, D_STATE), xc.dtype)
            _, ys = jax.lax.scan(step, h0, (dt.transpose(1, 0, 2), Bm.transpose(1, 0, 2), Cm.transpose(1, 0, 2), xc.transpose(1, 0, 2)))
            y = ys.transpose(1, 0, 2) + D_skip * xc
            y = y * jax.nn.silu(z)
            return y @ W_out
        mu = x.mean(-1, keepdims=True)
        var = x.var(-1, keepdims=True)
        xn = (x - mu) * jax.lax.rsqrt(var + LN_EPS) * gamma + beta
        out = _mamba_core(xn, W_in, conv_w, conv_b, W_x, W_dt, b_dt, A_log, D_skip, W_out)
        return x + out

    def _L2_ffn_ref(x, router_w, gate_w, up_w, down_w, shared_gate_w, shared_up_w, shared_down_w):
        import jax, jax.numpy as jnp
        import numpy as np
        B, S, H = (2, 64, 128)
        E, I = (64, 64)
        K = 8
        G, TG = (8, 4)
        SCALE = 2.5
        T = B * S
        CAP = 64

        def _moe_forward(x, router_w, gate_w, up_w, down_w, shared_gate_w, shared_up_w, shared_down_w):
            b, s, h = x.shape
            tokens = x.reshape(-1, h)
            t = tokens.shape[0]
            logits = tokens @ router_w
            scores = jax.nn.sigmoid(logits)
            eg = E // G
            group_scores = scores.reshape(t, G, eg).max(axis=-1)
            _, sel_groups = jax.lax.top_k(group_scores, TG)
            group_mask = jnp.zeros((t, G), bool).at[jnp.arange(t)[:, None], sel_groups].set(True)
            expert_mask = jnp.repeat(group_mask, eg, axis=1)
            masked_scores = jnp.where(expert_mask, scores, 0.0)
            topk_w, topk_idx = jax.lax.top_k(masked_scores, K)
            topk_w = topk_w / jnp.clip(topk_w.sum(-1, keepdims=True), 1e-09)
            topk_w = topk_w * SCALE
            flat_e = topk_idx.reshape(-1)
            onehot = jax.nn.one_hot(flat_e, E, dtype=jnp.int32)
            prior = jnp.cumsum(onehot, axis=0) - onehot
            pos = jnp.take_along_axis(prior, flat_e[:, None], axis=1)[:, 0]
            valid = (pos < CAP).astype(tokens.dtype)
            pos_c = jnp.minimum(pos, CAP - 1)
            tidx = jnp.repeat(jnp.arange(t), K)
            dispatch = jnp.zeros((E, CAP, h), tokens.dtype)
            dispatch = dispatch.at[flat_e, pos_c].add(tokens[tidx] * valid[:, None])
            g = jnp.einsum('ech,ehi->eci', dispatch, gate_w)
            u = jnp.einsum('ech,ehi->eci', dispatch, up_w)
            expert_out = jnp.einsum('eci,eih->ech', jax.nn.silu(g) * u, down_w)
            gathered = expert_out[flat_e, pos_c]
            contrib = gathered * (topk_w.reshape(-1) * valid)[:, None]
            output = jnp.zeros((t, h), tokens.dtype).at[tidx].add(contrib)
            sg = jax.nn.silu(tokens @ shared_gate_w) * (tokens @ shared_up_w)
            output = output + sg @ shared_down_w
            return output.reshape(b, s, h)
        return _moe_forward(x, router_w, gate_w, up_w, down_w, shared_gate_w, shared_up_w, shared_down_w)

    def _L3_attn_ref(x, Wk, bk, Wv, bv, ln_g, ln_b, Wo, bo):
        import jax, jax.numpy as jnp
        import numpy as np
        DIM = 128
        N_QUAT = DIM // 4
        LN_EPS = 1e-05
        NORM_EPS = 1e-12

        def quat_mul(q1, q2):
            r1, i1, j1, k1 = (q1[..., 0], q1[..., 1], q1[..., 2], q1[..., 3])
            r2, i2, j2, k2 = (q2[..., 0], q2[..., 1], q2[..., 2], q2[..., 3])
            r = r1 * r2 - i1 * i2 - j1 * j2 - k1 * k2
            i = r1 * i2 + i1 * r2 + j1 * k2 - k1 * j2
            j = r1 * j2 - i1 * k2 + j1 * r2 + k1 * i2
            k = r1 * k2 + i1 * j2 - j1 * i2 + k1 * r2
            return jnp.stack([r, i, j, k], axis=-1)

        def quat_conj(q):
            return q * jnp.array([1.0, -1.0, -1.0, -1.0], dtype=q.dtype)
        B, L, D = x.shape
        keys = (x @ Wk.T + bk).reshape(B, L, N_QUAT, 4)
        knorm = jnp.linalg.norm(keys, axis=-1, keepdims=True)
        keys = keys / jnp.maximum(knorm, NORM_EPS)
        values = (x @ Wv.T + bv).reshape(B, L, N_QUAT, 4)
        bound = quat_mul(values, keys)
        memory = jnp.cumsum(bound, axis=1)
        retrieved = quat_mul(memory, quat_conj(keys)).reshape(B, L, D)
        positions = jnp.arange(1, L + 1, dtype=x.dtype)
        retrieved = retrieved / jnp.sqrt(positions)[None, :, None]
        mu = jnp.mean(retrieved, axis=-1, keepdims=True)
        var = jnp.var(retrieved, axis=-1, keepdims=True)
        normed = (retrieved - mu) / jnp.sqrt(var + LN_EPS) * ln_g + ln_b
        return x + (normed @ Wo.T + bo)

    def _L3_ffn_ref(x, Wr, br, W_up, b_up, W_down, b_down):
        import jax, jax.numpy as jnp
        import numpy as np
        B, S, H = (4, 256, 128)
        E = 8
        GS = 2
        NG = E // GS
        F = int(H * 4 * (2.0 / 3.0))
        b, s, h = x.shape
        n_tok = b * s
        k = n_tok // E
        xf = x.reshape(n_tok, h)
        logits = xf @ Wr + br
        Sm = jax.nn.softmax(logits, axis=-1)
        G_t, idx_t = jax.lax.top_k(Sm.T, k)
        G = G_t.T
        idx = idx_t.T
        tokens = xf[idx]
        group = jnp.arange(E) // GS
        Wu = W_up[group]
        bu = b_up[group]
        mid = jax.nn.silu(jnp.einsum('keh,ehf->kef', tokens, Wu) + bu)
        out = jnp.einsum('kef,efh->keh', mid, W_down) + b_down
        y = jnp.zeros_like(xf).at[idx].add(G[..., None] * out)
        return y.reshape(b, s, h)
    x = L0_attn_x
    xn = _layernorm(x, axis=-1)
    s = _L0_attn_ref(xn, L0_attn_norm_w, L0_attn_in_proj_w, L0_attn_conv_w, L0_attn_conv_b, L0_attn_x_proj_w, L0_attn_dt_proj_w, L0_attn_dt_proj_b, L0_attn_A_log, L0_attn_D, L0_attn_out_proj_w)
    g = _silu(_L0_ffn_ref(xn, L0_ffn_Wqkv, L0_ffn_q_scale, L0_ffn_k_scale, L0_ffn_Wo, L0_ffn_ln_g, L0_ffn_ln_b, L0_ffn_W1, L0_ffn_b1, L0_ffn_W2, L0_ffn_b2))
    x = x + s * g
    xn = _layernorm(x, axis=-1)
    s = _L1_attn_ref(xn, L1_attn_Wq, L1_attn_Wk, L1_attn_Wv, L1_attn_Wlr, L1_attn_Wbeta, L1_attn_Wo, L1_attn_W_in_init, L1_attn_W_out_init)
    g = _silu(_L1_ffn_ref(xn, L1_ffn_wqkv, L1_ffn_q_scale, L1_ffn_k_scale, L1_ffn_wo, L1_ffn_ln_g, L1_ffn_ln_b, L1_ffn_w1, L1_ffn_b1, L1_ffn_w2, L1_ffn_b2))
    x = x + s * g
    xn = _layernorm(x, axis=-1)
    s = _L2_attn_ref(xn, L2_attn_gamma, L2_attn_beta, L2_attn_W_in, L2_attn_conv_w, L2_attn_conv_b, L2_attn_W_x, L2_attn_W_dt, L2_attn_b_dt, L2_attn_A_log, L2_attn_D_skip, L2_attn_W_out)
    g = _silu(_L2_ffn_ref(xn, L2_ffn_router_w, L2_ffn_gate_w, L2_ffn_up_w, L2_ffn_down_w, L2_ffn_shared_gate_w, L2_ffn_shared_up_w, L2_ffn_shared_down_w))
    x = x + s * g
    xn = _layernorm(x, axis=-1)
    s = _L3_attn_ref(xn, L3_attn_Wk, L3_attn_bk, L3_attn_Wv, L3_attn_bv, L3_attn_ln_g, L3_attn_ln_b, L3_attn_Wo, L3_attn_bo)
    g = _silu(_L3_ffn_ref(xn, L3_ffn_Wr, L3_ffn_br, L3_ffn_W_up, L3_ffn_b_up, L3_ffn_W_down, L3_ffn_b_down))
    x = x + s * g
    return x

_drawn_inputs = setup_inputs


def setup_inputs(seed=0):
    import zlib

    import numpy as np

    out = dict(_drawn_inputs(seed))
    spreads = {'L0_attn_norm_w': (1.0, 0.2),
     'L0_attn_conv_b': (0.0, 0.1),
     'L0_attn_dt_proj_b': (-4.600165843963623, 0.2),
     'L0_attn_D': (1.0, 0.2),
     'L0_ffn_q_scale': (1.0, 0.2),
     'L0_ffn_k_scale': (1.0, 0.2),
     'L0_ffn_ln_g': (1.0, 0.2),
     'L0_ffn_ln_b': (0.0, 0.1),
     'L0_ffn_b1': (0.0, 0.1),
     'L0_ffn_b2': (0.0, 0.1),
     'L1_ffn_q_scale': (1.0, 0.2),
     'L1_ffn_k_scale': (1.0, 0.2),
     'L1_ffn_ln_g': (1.0, 0.2),
     'L1_ffn_ln_b': (0.0, 0.1),
     'L1_ffn_b1': (0.0, 0.1),
     'L1_ffn_b2': (0.0, 0.1),
     'L2_attn_gamma': (1.0, 0.2),
     'L2_attn_beta': (0.0, 0.1),
     'L2_attn_conv_b': (0.0, 0.1),
     'L2_attn_D_skip': (1.0, 0.2),
     'L3_attn_bk': (0.0, 0.1),
     'L3_attn_bv': (0.0, 0.1),
     'L3_attn_ln_g': (1.0, 0.2),
     'L3_attn_ln_b': (0.0, 0.1),
     'L3_attn_bo': (0.0, 0.1),
     'L3_ffn_br': (0.0, 0.1)}
    factors = {}
    for name, (base, spread) in spreads.items():
        noise = np.random.default_rng([zlib.crc32(name.encode()), seed]).standard_normal(out[name].shape)
        drawn = base * np.exp(spread * noise) if base else spread * noise
        out[name] = jnp.asarray(drawn.astype(out[name].dtype))
    for name, factor in factors.items():
        out[name] = (out[name] * factor).astype(out[name].dtype)
    return out
```

```python
from contextlib import ExitStack, contextmanager

import numpy as np

import concourse.bass as bass
from concourse import mybir

F32 = mybir.dt.float32
BF16 = mybir.dt.bfloat16
I32 = mybir.dt.int32
ALU = mybir.AluOpType
ACT = mybir.ActivationFunctionType
AX = mybir.AxisListType

P = 128
C = 128
BATCH, SEQ = 8, 512
TT = SEQ // P
NT = BATCH * TT
EPS = 1e-5
DH = 64
QK_SCALE = 8.0
MASKED = -1e30


class Wait(tuple):
    pass


def furthest(*waits):
    last = {}
    for w in waits:
        n = w[0].name
        if n not in last or w.offset > last[n].offset:
            last[n] = w
    return list(last.values())


class Count:

    def __init__(self, sem, keys, past=None):
        self.sem, self.keys, self.past = sem, list(keys), past
        self.per = len(self.keys)
        self.index = {k: i for i, k in enumerate(self.keys)}
        assert len(self.index) == self.per

    def __call__(self, it, key, back=0):
        if self.past and (key not in self.index or self.per + self.index[key] < back):
            wait = Wait((self.past, 1))
            wait.offset = 1
            return wait
        assert back <= self.per
        offset = self.per + self.index[key] + 1 - back
        wait = Wait((self.sem, it * self.per + offset))
        wait.offset = offset
        return wait


class Banks:

    def __init__(self, sem, name, tensors, keys, past=None):
        n = len(tensors)
        assert (past or len(keys) % n == 0) and len(set(keys)) == len(keys)
        self.tensors = tensors
        self.where = {k: i % n for i, k in enumerate(keys)}
        self.full = [Count(sem(f"{name}{i}_full"), keys[i::n], past) for i in range(n)]
        self.empty = [Count(sem(f"{name}{i}_empty"), keys[i::n], past) for i in range(n)]

    def at(self, key):
        return self.tensors[self.where[key]]

    def free(self, it, key):
        return self.empty[self.where[key]](it, key, 1)

    def written(self, it, key, ago=0):
        s = self.full[self.where.get(key, 0)]
        return s(it, key, ago * s.per)

    def read(self, it, key, ago=0):
        s = self.empty[self.where.get(key, 0)]
        return s(it, key, ago * s.per)

    def last_in_banks(self, keys):
        last = {}
        for k in keys:
            if k in self.where:
                b = self.where[k]
                if b not in last or self.empty[b].index[k] > self.empty[b].index[last[b]]:
                    last[b] = k
        return last.values()

    def all_read(self, it, keys, ago=0):
        return [self.read(it, k, ago) for k in self.last_in_banks(keys)]

    def all_written(self, it, keys, ago=0):
        return [self.written(it, k, ago) for k in self.last_in_banks(keys)]

    def full_of(self, key):
        return self.full[self.where[key]].sem

    def empty_of(self, key):
        return self.empty[self.where[key]].sem


class Room:

    def __init__(self, nc, ctx, name):
        self.nc, self.ctx, self.name, self.sems, self.counts = nc, ctx, name, [], []
        self.programs, self.past = ExitStack(), None

    def block(self):
        return self.programs.enter_context(self.nc.Block())

    def sb(self, name, shape, dt=F32):
        return self.ctx.enter_context(self.nc.sbuf_tensor(f"{self.name}_{name}", shape, dt))

    def ps(self, name, shape, dt=F32):
        return self.ctx.enter_context(self.nc.psum_tensor(f"{self.name}_{name}", shape, dt))

    def sem(self, name):
        s = self.ctx.enter_context(self.nc.semaphore(f"{self.name}_{name}"))
        self.sems.append(s)
        return s

    def count(self, name, keys):
        s = Count(self.sem(name), keys, self.past)
        self.counts.append(s)
        return s

    def banks(self, name, tensors, keys):
        b = Banks(self.sem, name, tensors, keys, self.past)
        self.counts += b.full + b.empty
        return b

    def give_credit(self, eng):
        if self.past:
            eng.sem_inc(self.past, 1)
        for s in self.counts:
            if s.per:
                eng.sem_inc(s.sem, s.per)


@contextmanager
def stage(nc, name):
    with ExitStack() as ctx:
        room = Room(nc, ctx, name)
        yield room
        room.programs.close()
        for s in room.sems:
            nc.gpsimd.sem_clear(s)
        nc.all_engine_barrier()


def spread(ap, dim, n):
    shape = list(ap.shape)
    shape.insert(dim, n)
    return ap.unsqueeze(dim).broadcast_to(shape)


def shape_constants():
    f = np.float32
    eye = np.eye(P, dtype=f)
    out = {
        "ident": eye,
        "down1": np.eye(P, k=1, dtype=f),
        "last1": np.zeros((P, P), f),
        "ones": np.ones((P, P), f),
        "before": np.triu(np.ones((P, P), f), 1),
        "upto": np.triu(np.ones((P, P), f), 0),
    }
    out["last1"][P - 1, 0] = 1.0
    return out


def rotary_constants(window):
    f = np.float32
    half = np.arange(0, DH, 2).astype(f)
    inv_freq = (f(1.0) / np.power(f(10000.0), half / f(DH))).astype(f)
    t = np.arange(SEQ).astype(f)
    freqs = (t[:, None] * inv_freq[None, :]).astype(f)
    base = (half + f(0.4 * DH)) / f(1.4 * DH)
    scale = np.power(base[None, :], ((t - f(SEQ // 2)) / f(window // 2))[:, None]).astype(f)
    cos, sin = np.cos(freqs).astype(f), np.sin(freqs).astype(f)
    full = lambda a, b: np.concatenate([a, b], 1)
    tabs = [full(cos, cos) * full(scale, scale), full(-sin, sin) * full(scale, scale),
            full(cos, cos) / full(scale, scale), full(-sin, sin) / full(scale, scale)]
    tabs = np.stack(tabs, 0).reshape(4, TT, P, DH)
    return np.ascontiguousarray(tabs.transpose(2, 0, 1, 3)).astype(f)


def window_mask(window):
    i = np.arange(P)[:, None]
    j = np.arange(-window, P)[None, :]
    seen = (j <= i) & (j >= i - window)
    both = np.stack([seen & (j >= 0), seen], 1)
    both = np.concatenate([both[:, :, window:], both[:, :, :window], both], 2)
    return np.where(both, 0.0, MASKED).astype(mybir.dt.np(BF16))


def by_partition(a, p=P):
    n = -(-a.shape[-2] // p)
    full = np.zeros(a.shape[:-2] + (n * p, a.shape[-1]), a.dtype)
    full[..., :a.shape[-2], :] = a
    full = full.reshape(a.shape[:-2] + (n, p, a.shape[-1]))
    return np.ascontiguousarray(np.moveaxis(full, -3, -2))


def lay_out_attention(inputs, prefix, names):
    get = {k: np.asarray(inputs[f"{prefix}_{v}"]) for k, v in names.items()}
    depth, hid2 = get["b1"].shape
    b1 = by_partition(get["b1"].reshape(depth, 2, hid2 // 2, 1))
    return {
        "wqkv": get["wqkv"],
        "wo": by_partition(get["wo"]),
        "w1": get["w1"],
        "w2": by_partition(get["w2"]),
        "b1": np.ascontiguousarray(b1[..., 0].transpose(0, 2, 1, 3)),
        "b2": get["b2"],
        "ln": np.ascontiguousarray(np.stack([get["ln_g"], get["ln_b"]], 2)),
        "scales": np.ascontiguousarray(np.stack([get["q_scale"], get["k_scale"]], 1).reshape(depth, -1)),
    }


def lay_out_mamba(inputs, prefix, names):
    get = {k: np.asarray(inputs[f"{prefix}_{v}"]) for k, v in names.items() if v}
    model = get["w_in"].shape[0]
    gain = get["gain"].reshape(model, 1)
    shift = get["shift"].reshape(model, 1) if "shift" in get else np.zeros_like(gain)
    cols = np.concatenate([get["conv_w"], get["conv_b"][:, None], get["b_dt"][:, None], get["skip"][:, None]], 1)
    return {
        "w_in": get["w_in"], "w_x": by_partition(get["w_x"]), "w_dt": get["w_dt"], "w_out": by_partition(get["w_out"]),
        "cols": by_partition(cols), "ln": np.ascontiguousarray(np.concatenate([gain, shift], 1)),
        "a_log": by_partition(get["a_log"]),
    }


MAMBA_NAMES = {
    "L0_attn": dict(w_in="in_proj_w", conv_w="conv_w", conv_b="conv_b", w_x="x_proj_w", w_dt="dt_proj_w", b_dt="dt_proj_b",
                    a_log="A_log", skip="D", w_out="out_proj_w", gain="norm_w"),
    "L2_attn": dict(w_in="W_in", conv_w="conv_w", conv_b="conv_b", w_x="W_x", w_dt="W_dt", b_dt="b_dt", a_log="A_log",
                    skip="D_skip", w_out="W_out", gain="gamma", shift="beta"),
}
ATTENTION_NAMES = {
    "L0_ffn": dict(wqkv="Wqkv", wo="Wo", w1="W1", b1="b1", w2="W2", b2="b2", ln_g="ln_g", ln_b="ln_b", q_scale="q_scale",
                   k_scale="k_scale"),
    "L1_ffn": dict(wqkv="wqkv", wo="wo", w1="w1", b1="b1", w2="w2", b2="b2", ln_g="ln_g", ln_b="ln_b", q_scale="q_scale",
                   k_scale="k_scale"),
}


def lay_out_ttt(inputs):
    get = lambda n: np.asarray(inputs[f"L1_attn_{n}"])
    cont = np.ascontiguousarray
    H, N = 16, 64
    win, wout = get("W_in_init")[0], get("W_out_init")[0]
    pairs = lambda a: cont(a.reshape(N, H // 2, 2, N))
    base = np.concatenate([np.full((2 * H, 1), 0.001 / 64), np.full((2 * H, 1), 0.9 / 64)]).astype(np.float32)
    return {
        "wq": cont(get("Wq").T), "wk": cont(get("Wk").T), "wv": cont(get("Wv").T),
        "wo": by_partition(cont(get("Wo").T)),
        "w_rates": cont(np.concatenate([get("Wlr"), get("Wbeta")]).T), "base": base,
        "win_t": cont(pairs(win).transpose(2, 3, 1, 0).reshape(P, H // 2, N)),
        "wout": cont(pairs(wout).transpose(2, 0, 1, 3).reshape(P, H // 2, N)),
        "wout_t": cont(pairs(wout).transpose(2, 3, 1, 0).reshape(P, H // 2, N)),
    }


def lay_out_moe(inputs):
    get = lambda n: np.asarray(inputs[f"L2_ffn_{n}"])
    cont = np.ascontiguousarray
    E, I = 64, 64
    two = lambda a: cont(a.reshape(E // 2, 2, C, I).transpose(2, 0, 1, 3).reshape(C, E // 2, 2 * I))
    return {"router": get("router_w"), "wg": two(get("gate_w")), "wu": two(get("up_w")),
            "wd": cont(get("down_w").reshape(E // 2, 2 * I, C).transpose(1, 0, 2)),
            "sg": get("shared_gate_w"), "su": get("shared_up_w"), "sd": get("shared_down_w")}


def lay_out_route(inputs):
    get = lambda n: np.asarray(inputs[f"L3_ffn_{n}"])
    cont = np.ascontiguousarray
    wd = by_partition(get("W_down"))
    return {"wr": get("Wr"), "br": get("br").reshape(1, -1), "wu": cont(get("W_up").transpose(1, 0, 2)),
            "bu": cont(by_partition(get("b_up")[..., None])[..., 0].transpose(1, 0, 2)),
            "wd": cont(wd.reshape(4, 2, P, wd.shape[2], C).transpose(2, 3, 0, 1, 4).reshape(P, wd.shape[2], 4, 2 * C)),
            "bd": get("b_down")}


def lay_out_quat(inputs):
    get = lambda n: np.asarray(inputs[f"L3_attn_{n}"])
    cont = np.ascontiguousarray
    by_comp = lambda a: cont(a.reshape((C // 4, 4) + a.shape[1:]).swapaxes(0, 1).reshape(a.shape))
    rows = np.concatenate([by_comp(get("bk")), by_comp(get("bv")), get("bo")]).reshape(1, 3 * C)
    position = np.arange(1, SEQ + 1).astype(np.float32)
    return {"wk": cont(by_comp(get("Wk")).T), "wv": cont(by_comp(get("Wv")).T), "wo": by_comp(cont(get("Wo").T)),
            "rows": cont(rows), "ln": cont(np.stack([by_comp(get("ln_g")), by_comp(get("ln_b"))], 1)),
            "isq": cont((1.0 / np.sqrt(position)).astype(np.float32).reshape(TT, P).T)}


def local_attention_net(nc, g, name, heads, window, depth, w):
    inner = heads * DH
    n_chunks = inner // 512
    pairs = heads // 2
    keys = window + P
    hid = w["w1"].shape[2] // 2
    hid_chunks = [(o, min(P, hid - o)) for o in range(0, hid, P)]
    nhc = len(hid_chunks)

    def early(tt):
        return [("proj", tt, "q", 0), ("proj", tt, "k", 0)]

    def turns_of(tt, chunks):
        return [("turn", tt, what, c) for c in chunks for what in "qk"]

    def late(tt):
        steps = []
        for c in range(1, n_chunks):
            steps += [("proj", tt, "q", c), ("proj", tt, "k", c)]
            if c == 1:
                steps += turns_of(tt, [0])
        return steps + [("proj", tt, "v", c) for c in range(n_chunks)]

    def last_turns(tt):
        return turns_of(tt, range(1 if n_chunks > 1 else 0, n_chunks)) + [("kcarry", tt)]

    def attend_steps(tt):
        steps = [("score", tt, 0), ("score", tt, 1)]
        for j in range(pairs):
            steps.append(("flip", tt, j))
            if j + 2 < pairs:
                steps.append(("score", tt, j + 2))
            if j:
                steps.append(("value", tt, j - 1))
        steps.append(("value", tt, pairs - 1))
        return steps

    def merged(a, b):
        out, done = [], 0
        for i, s in enumerate(a):
            out.append(s)
            upto = (i + 1) * len(b) // len(a)
            out += b[done:upto]
            done = upto
        return out

    def finish_steps(tt):
        return [("oturn", tt, u) for u in range(pairs // 4)] + [("out", tt)]

    START = [("layer",), ("shift",)]
    FEED = ([("fshift",), ("rstd",), ("xn",), ("fturn",)] + [("gate", c) for c in range(nhc)] + [("up", c) for c in range(nhc)] +
            [("down",)])
    gates, ups = FEED[4:4 + nhc], FEED[4 + nhc:]
    SIDE = [merged(late(1) + early(2) + last_turns(1), FEED[:2]),
            merged(late(2) + early(3) + last_turns(2), FEED[2:4]),
            [("fetch",)] + late(3)[:-1] + gates + late(3)[-1:] + START + early(0) + last_turns(3),
            merged(late(0) + early(1) + last_turns(0), ups)]
    DELAY = 2
    MAIN, TAIL = [], pairs // 2 if n_chunks > 1 else 0
    for tt in range(TT):
        first, rest = attend_steps(tt)[:3], attend_steps(tt)[3:]
        turns = finish_steps((tt - 1) % TT)
        MAIN += first[:2] + turns[:-1] + first[2:] + rest[:1] + turns[-1:] + merged(rest[1:len(rest) - TAIL], SIDE[tt]) + rest[len(rest) - TAIL:]
        MAIN.append(("vcarry", (tt + 1) % TT))
    if TAIL:
        for tt in range(1, TT):
            for j in range(2):
                MAIN.remove(("score", tt, j))
                MAIN.insert(MAIN.index(("value", tt - 1, pairs - 2 + j)), ("score", tt, j))
    MAIN.append(("end",))
    BEFORE = [("fetch",)] + START + early(0) + late(0) + early(1) + last_turns(0) + [("vcarry", 0)]
    AFTER = finish_steps(TT - 1) + FEED

    def lag(step):
        if step[0] in ("fetch", "layer", "shift") or step[0] in ("proj", "turn", "kcarry", "vcarry") and step[1] == 0 or step in early(1):
            return -1
        if step[0] in ("oturn", "out") and step[1] == TT - 1 or step in FEED:
            return 1
        return 0

    def ago(step, other, sequences=0):
        n = lag(step) - lag(other) + sequences
        assert 0 <= n <= 1
        return n

    def sequence(step, b):
        return b if lag(step) == 0 else (b - lag(step)) % BATCH

    CHUNKS = [s for s in MAIN if s[0] == "proj" and s[2] != "v"]
    def later(steps, n):
        place = [i + (n + 0.5 if s in CHUNKS else 0) for i, s in enumerate(steps)]
        return [steps[i] for i in sorted(range(len(steps)), key=lambda i: place[i])]

    RING = ("shift", "proj", "turn", "oturn", "out", "fshift", "fturn", "gate", "up", "down")

    with ExitStack() as ctx:
        r = Room(nc, ctx, name)
        wqkv = r.sb("wqkv", [P, 3 * inner])
        wo = r.sb("wo", [P, pairs, C])
        w1 = r.sb("w1", [P, 2 * hid])
        w2 = r.sb("w2", [P, nhc, C])
        b1 = r.sb("b1", [P, 2, nhc])
        b2 = r.sb("b2", [P, C])
        ln = r.sb("ln", [P, 2])
        scales = r.sb("scales", [P, 2 * DH])
        rope = r.sb("rope", [P, 4, TT, DH])
        table = r.sb("table", [P, 4, TT, DH])
        mask = r.sb("mask", [P, 2, 2 * keys], BF16)
        xb = r.sb("xb", [P, TT + 1, C])
        hT = r.sb("hT", [P, SEQ])
        QN = 4
        qs = r.sb("qs", [P, QN, 8, DH])
        sq = r.sb("sq", [P, QN, 8, DH])
        m1 = r.sb("m1", [P, 2, 8, DH])
        m2 = r.sb("m2", [P, 2, 8, DH])
        ssq = r.sb("ssq", [P, 2, 8])
        rn = r.sb("rn", [P, 2, 8])
        qn = r.sb("qn", [P, QN, 8, DH])
        qT = r.sb("qT", [P, 2, 2, pairs, P])
        kT = r.sb("kT", [P, 2, pairs, window + P + window])
        vb = r.sb("vb", [P, 2, heads, DH + 1])
        vprev = r.sb("vprev", [P, 2, heads, DH + 1])
        nmx = r.sb("nmx", [P, 2, 2])
        prob = r.sb("prob", [P, 2, 2 * keys])
        pT = r.sb("pT", [P, 2, 2, P])
        pTprev = r.sb("pTprev", [P, 2, P])
        rec = r.sb("rec", [P, 4])
        o_sb = r.sb("o_sb", [P, heads, DH])
        oT = r.sb("oT", [P, pairs, P])
        stats = r.sb("stats", [P, TT, 6])
        mv = r.sb("mv", [P, TT, 2])
        rstd = r.sb("rstd", [P, TT])
        xn = r.sb("xn", [P, TT, C])
        hnT = r.sb("hnT", [P, SEQ])
        gate = r.sb("gate", [P, nhc, SEQ])
        hh = r.sb("hh", [P, nhc, SEQ])
        y = r.sb("y", [P, TT, C])
        eps = r.sb("eps", [P, TT])
        half = r.sb("half", [P, TT * 8])
        ring_ps = [r.ps("ring0", [P, 512]), r.ps("ring1", [P, 512])]
        s_ps = r.ps("scores", [P, 2, 512])
        pt_ps = r.ps("pt", [P, 2, 4, P])
        o_ps = r.ps("o", [P, 2, 512])

        def programs(r, STEPS):
            main = STEPS is MAIN
            if main and len([s for s in STEPS if s[0] in RING]) % 2:
                raise ValueError("an odd number of uses")
            uses = [s for s in STEPS if s[0] in RING]
            QK = [s for s in STEPS if s[0] == "proj" and s[2] != "v"]
            PAIRS = [s[1:] for s in MAIN if s[0] == "value"] if main else []
            if not main:
                r.past = r.sem("past")
            ring = r.banks("ring", ring_ps, uses)
            loaded = r.sem("loaded")
            qkv_ready = r.sem("qkv_ready")
            wo_ready = r.sem("wo_ready")
            feed_ready = r.sem("feed_ready")
            zeroed = r.sem("zeroed")
            table_ready = r.sem("table_ready")
            passed = r.sem("passed")
            xb_ready = r.count("xb_ready", [s for s in STEPS if s[0] == "fetch"])
            rotated = r.count("rotated", QK)
            normed = r.count("normed", QK)
            kcarried = r.count("kcarried", [s for s in STEPS if s[0] == "kcarry"])
            vcarried = r.count("vcarried", [s for s in STEPS if s[0] == "vcarry"])
            scored = r.count("scored", PAIRS)
            maxed = r.count("maxed", PAIRS)
            exped = r.count("exped", PAIRS)
            flipped = r.count("flipped", PAIRS)
            unflipped = [r.count(f"unflipped_{who}", [k for k in PAIRS if k[1] % 2 == s])
                         for s, who in enumerate(("dve", "act"))]
            valued = r.count("valued", PAIRS)
            o_ready = r.count("o_ready", [(tt, j) for tt, j in PAIRS if j % 2])
            fed = [s for s in STEPS if s == ("down",)]
            varied = r.count("varied", fed)
            rstd_ready = r.count("rstd_ready", fed)
            xn_ready = r.count("xn_ready", fed)
            x2_ready = r.count("x2_ready", fed)
            FEED_DMAS = 5
            last_v = n_chunks - 1

            def go_round(e, body):
                if not main:
                    body(e, 0, -1 if STEPS is BEFORE else BATCH, None, True)
                    return
                with e.Fori(0, depth) as l:
                    with e.Fori(0, BATCH - 1) as b:
                        body(e, l * BATCH + b, b, l, False)
                    body(e, l * BATCH + BATCH - 1, BATCH - 1, l, True)

            block = r.block()

            @block.sync
            def _(e):
                r.give_credit(e)

                def load_qkv(one, *sem):
                    e.dma_start(wqkv[:], w["wqkv"][one].rearrange("o c n -> c (o n)")).then_inc(qkv_ready, 16)
                    e.dma_start(scales[:], w["scales"][one].broadcast_to([P, 2 * DH])).then_inc(qkv_ready, 16)
                if STEPS is BEFORE:
                    e.dma_start(rope[:], w["rope"]).then_inc(loaded, 16)
                    e.dma_start(mask[:], w["mask"]).then_inc(loaded, 16)
                    e.dma_start(ln[:], w["ln"][0:1].rearrange("o p a -> p (o a)")).then_inc(loaded, 16)
                    load_qkv(slice(0, 1))
                    e.wait_ge(loaded, 48)
                if not main:
                    return
                flat = lambda t: t.rearrange("o p a b -> p (o a) b")
                with e.Fori(0, depth) as l:
                    one = bass.ds(l, 1)
                    first, last = l * BATCH, l * BATCH + BATCH - 1
                    e.wait_ge(*ring.written(first, ("out", TT - 1)))
                    e.sem_inc(passed, 1)
                    e.dma_start(wo[:], flat(w["wo"][one])).then_inc(wo_ready, 16)
                    e.wait_ge(*x2_ready(first, ("down",)))
                    e.sem_inc(passed, 1)
                    e.dma_start(w1[:], w["w1"][one].rearrange("o c n -> c (o n)")).then_inc(feed_ready, 16)
                    e.dma_start(w2[:], flat(w["w2"][one])).then_inc(feed_ready, 16)
                    e.dma_start(b1[:], flat(w["b1"][one])).then_inc(feed_ready, 16)
                    e.dma_start(b2[:], w["b2"][one].broadcast_to([P, C])).then_inc(feed_ready, 16)
                    e.dma_start(ln[:], w["ln"][one].rearrange("o p a -> p (o a)")).then_inc(feed_ready, 16)
                    for done in ring.all_written(last, [s for s in uses if s[0] == "proj" and s[1] == TT - 1]):
                        e.wait_ge(*done)
                        e.sem_inc(passed, 1)
                    load_qkv(bass.ds((l + 1) % depth, 1))

            @block.gpsimd
            def _(e):
                if STEPS is BEFORE:
                    for t in (xb[:, 0, :], qT[:], kT[:], vb[:], vprev[:], w1[:], w2[:], b1[:], b2[:], wo[:], o_sb[:]):
                        e.memset(t, 0.0)
                    e.memset(half[:], -0.5)
                    e.memset(eps[:], EPS)
                    e.drain()
                    e.memset(vb[:, :, :, DH:DH + 1], 1.0)
                    e.drain().then_inc(zeroed, 1)

                def body(e, it, b, l, last):
                    for step in STEPS:
                        kind = step[0]
                        if kind == "fetch":
                            e.wait_ge(*x2_ready(it, ("down",), x2_ready.per))
                            e.wait_ge(*ring.written(it, ("shift",), 1))
                            e.sem_inc(passed, 1)
                            e.tensor_copy(xb[:, 1:, :],
                                          g.f[:, bass.ds(sequence(step, b) * TT, TT), :]).then_inc(xb_ready.sem, 1)
                        elif kind == "layer" and last:
                            e.wait_ge(table_ready, 1 if l is None else l + 1)
                            e.sem_inc(passed, 1)
                        elif kind == "proj" and step[2] != "v":
                            q = CHUNKS.index(step)
                            s = q % 2
                            cos = table[:, 0 if step[2] == "q" else 2, step[1]]
                            e.wait_ge(*ring.read(it, step))
                            e.tensor_tensor(m1[:, s], qs[:, q % QN], spread(cos, 1, 8), ALU.mult)
                            e.drain()
                            e.wait_ge(*rotated(it, step))
                            e.tensor_tensor(m1[:, s], m1[:, s], m2[:, s], ALU.add)
                            e.tensor_scalar(rn[:, s], ssq[:, s], 1e-24, None, ALU.max)
                            e.drain()
                            e.tensor_tensor(rn[:, s], rn[:, s], half[:, 0:8], ALU.pow)
                            e.drain()
                            turn = ("turn",) + CHUNKS[q - QN][1:]
                            e.wait_ge(*ring.written(it, turn, 0 if MAIN.index(turn) < MAIN.index(step) else 1))
                            e.tensor_tensor(qn[:, q % QN], m1[:, s], spread(rn[:, s], 2, DH), ALU.mult).then_inc(normed.sem, 1)
                        elif kind == "rstd":
                            e.wait_ge(*varied(it, ("down",)))
                            e.tensor_tensor(rstd[:], mv[:, :, 1], eps[:], ALU.add)
                            e.drain()
                            e.tensor_tensor(rstd[:], rstd[:], half[:, 0:TT], ALU.pow).then_inc(rstd_ready.sem, 1)
                go_round(e, body)

            @block.scalar
            def _(e):
                def body(e, it, b, l, last):
                    for step in STEPS:
                        kind = step[0]
                        if kind == "shift":
                            for done in ring.all_written(it, [s for s in uses if s[0] == "proj" and s[1] == TT - 1]):
                                e.wait_ge(*done)
                            e.wait_ge(*ring.written(it, step))
                            e.activation(hT[:], ring.at(step)[:], ACT.Copy).then_inc(ring.empty_of(step), 1)
                        elif kind == "proj" and step[2] != "v":
                            s = CHUNKS.index(step) % QN
                            e.wait_ge(*normed(it, step, QN))
                            e.wait_ge(*ring.written(it, step))
                            e.activation(sq[:, s], ring.at(step)[:], ACT.Square)
                            e.activation(qs[:, s], ring.at(step)[:], ACT.Copy).then_inc(ring.empty_of(step), 1)
                        elif kind == "proj":
                            tt, c = step[1], step[3]
                            if c == 0:
                                e.wait_ge(*valued(it, ((tt - 2) % TT, pairs - 1), len(PAIRS) if tt == 1 else 0))
                                e.wait_ge(*vcarried(it, ("vcarry", tt), 2))
                            e.wait_ge(*ring.written(it, step))
                            e.activation(vb[:, tt % 2, 8 * c:8 * c + 8, 0:DH],
                                         ring.at(step).rearrange("p (h d) -> p h d", h=8), ACT.Copy).then_inc(ring.empty_of(step), 1)
                        elif kind == "turn" and step[2] == "q":
                            tt, c = step[1], step[3]
                            e.wait_ge(*ring.written(it, step))
                            for h in range(2):
                                rows = slice(h * DH, h * DH + DH)
                                a = e.activation(qT[rows, tt % 2, h, 4 * c:4 * c + 4, :],
                                                 ring.at(step)[rows].rearrange("p (h d) -> p h d", h=4), ACT.Copy)
                            a.then_inc(ring.empty_of(step), 1)
                        elif kind == "score":
                            key = step[1:]
                            s = key[1] % 2
                            e.wait_ge(*flipped(it, key, 2))
                            e.wait_ge(*maxed(it, key))
                            for h in range(2):
                                a = e.activation(prob[:, s, h * keys:(h + 1) * keys], s_ps[:, s, h * keys:(h + 1) * keys], ACT.Exp,
                                                 bias=nmx[:, s, h:h + 1])
                            a.then_inc(exped.sem, 1)
                        elif kind == "flip":
                            key = step[1:]
                            s = key[1] % 2
                            if s == 0:
                                continue
                            e.wait_ge(*valued(it, key, 2))
                            e.wait_ge(*flipped(it, key))
                            e.activation(pTprev[0:2 * window, s], pt_ps[0:2 * window, s, 2], ACT.Copy)
                            e.activation(pT[:, s], pt_ps[:, s, 0:2], ACT.Copy).then_inc(unflipped[1].sem, 1)
                        elif kind == "kcarry":
                            tt = step[1]
                            if tt == TT - 1:
                                e.drain().then_inc(kcarried.sem, 1)
                                continue
                            p, q = tt % 2, 1 - tt % 2
                            for done in ring.all_read(it, [s for s in uses if s[:3] == ("turn", tt, "k")]):
                                e.wait_ge(*done)
                            e.wait_ge(*scored(it, ((tt - 1) % TT, pairs - 1)))
                            e.activation(kT[:, q, :, 0:window], kT[:, p, :, P:P + window], ACT.Copy)
                            e.activation(kT[:, q, :, keys:keys + window], kT[:, p, :, P:P + window],
                                         ACT.Copy).then_inc(kcarried.sem, 1)
                        elif kind == "oturn":
                            tt, u = step[1:]
                            before = ("out", (tt - 1) % TT)
                            e.wait_ge(*ring.written(it, before, ago(step, before, 0 if tt else 1)))
                            e.wait_ge(*ring.written(it, step))
                            e.activation(oT[:, 4 * u:4 * u + 4, :],
                                         ring.at(step).rearrange("p (h d) -> p h d", h=4), ACT.Copy).then_inc(ring.empty_of(step), 1)
                        elif kind == "fturn":
                            e.wait_ge(*ring.written(it, ("up", nhc - 1), 1))
                            e.wait_ge(*ring.written(it, step))
                            e.activation(hnT[:], ring.at(step)[:], ACT.Identity, bias=ln[:, 1:2],
                                         scale=ln[:, 0:1]).then_inc(ring.empty_of(step), 1)
                        elif kind == "gate":
                            c = step[1]
                            n = hid_chunks[c][1]
                            e.wait_ge(*ring.read(it, ("up", c), 1))
                            e.wait_ge(*ring.written(it, step))
                            e.activation(gate[0:n, c], ring.at(step)[0:n], ACT.Gelu,
                                         bias=b1[0:n, 1, c:c + 1]).then_inc(ring.empty_of(step), 1)
                        elif kind == "end":
                            e.wait_ge(feed_ready, (l + 1) * (16 * FEED_DMAS))
                            e.sem_inc(passed, 1)
                go_round(e, body)

            @block.vector
            def _(e):
                def body(e, it, b, l, last):
                    for step in later(STEPS, DELAY):
                        kind = step[0]
                        if kind == "layer" and last:
                            if l is None:
                                e.wait_ge(loaded, 48)
                            e.wait_ge(qkv_ready, 32 if l is None else (l + 1) * 32)
                            e.wait_ge(*normed(it, ("proj", TT - 1, "k", n_chunks - 1)))
                            for qk in range(2):
                                f = QK_SCALE if qk == 0 else 1.0
                                sc = scales[:, qk * DH:(qk + 1) * DH]
                                h2 = DH // 2
                                e.scalar_tensor_tensor(table[:, 2 * qk], rope[:, 2 * qk], f, spread(sc, 1, TT),
                                                       ALU.mult, ALU.mult)
                                for o, i in ((0, h2), (h2, 0)):
                                    e.scalar_tensor_tensor(table[:, 2 * qk + 1, :, o:o + h2], rope[:, 2 * qk + 1, :, o:o + h2],
                                                           f, spread(sc[:, i:i + h2], 1, TT), ALU.mult, ALU.mult)
                            e.drain().then_inc(table_ready, 1)
                        elif kind == "proj" and step[2] != "v":
                            tt = step[1]
                            s = CHUNKS.index(step) % 2
                            t = 0 if step[2] == "q" else 2
                            sin = table[:, t + 1, tt]
                            h2 = DH // 2
                            e.wait_ge(*ring.read(it, step))
                            e.wait_ge(*normed(it, step, 2))
                            src = qs[:, CHUNKS.index(step) % QN]
                            e.tensor_tensor(m2[:, s, :, 0:h2], src[:, :, h2:DH], spread(sin[:, 0:h2], 1, 8), ALU.mult)
                            e.tensor_tensor(m2[:, s, :, h2:DH], src[:, :, 0:h2], spread(sin[:, h2:DH], 1, 8), ALU.mult)
                            e.tensor_reduce(ssq[:, s], sq[:, CHUNKS.index(step) % QN], AX.X, ALU.add).then_inc(rotated.sem, 1)
                        elif kind == "turn" and step[2] == "k":
                            tt, c = step[1], step[3]
                            e.wait_ge(*kcarried(it, ("kcarry", tt), 2))
                            e.wait_ge(*ring.written(it, step))
                            e.tensor_copy(kT[:, tt % 2, 4 * c:4 * c + 4, window:keys],
                                          ring.at(step).rearrange("p (h d) -> p h d", h=4)).then_inc(ring.empty_of(step), 1)
                        elif kind == "score":
                            key = step[1:]
                            s = key[1] % 2
                            e.wait_ge(*exped(it, key, 2))
                            e.wait_ge(*scored(it, key))
                            e.tensor_reduce(nmx[:, s], s_ps[:, s, 0:2 * keys].rearrange("p (h k) -> p h k", h=2), AX.X, ALU.max,
                                            negate=True).then_inc(maxed.sem, 1)
                        elif kind == "flip":
                            key = step[1:]
                            s = key[1] % 2
                            if s == 1:
                                continue
                            e.wait_ge(*valued(it, key, 2))
                            e.wait_ge(*flipped(it, key))
                            e.tensor_copy(pTprev[0:2 * window, s], pt_ps[0:2 * window, s, 2])
                            e.tensor_copy(pT[:, s], pt_ps[:, s, 0:2]).then_inc(unflipped[0].sem, 1)
                        elif kind == "value" and step[2] % 2:
                            tt, j = step[1:]
                            e.wait_ge(*valued(it, (tt, j)))
                            if j == 1:
                                prev = ("oturn", (tt - 1) % TT, pairs // 4 - 1)
                                e.wait_ge(*ring.written(it, prev))
                                if pairs > 4:
                                    e.wait_ge(*ring.written(it, ("oturn", (tt - 1) % TT, 0)))
                            o = o_ps[:, (j // 2) % 2, 0:4 * (DH + 1)].rearrange("p (h d) -> p h d", h=4)
                            e.reciprocal(rec[:], o[:, :, DH])
                            e.drain()
                            e.tensor_tensor(o_sb[:, 2 * j - 2:2 * j + 2, :], o[:, :, 0:DH], spread(rec[:], 2, DH),
                                            ALU.mult).then_inc(o_ready.sem, 1)
                            e.drain()
                        elif kind == "vcarry":
                            tt = step[1]
                            if tt == TT - 1:
                                e.drain().then_inc(vcarried.sem, 1)
                                continue
                            for done in ring.all_read(it, [s for s in uses if s[:3] == ("proj", tt, "v")]):
                                e.wait_ge(*done)
                            e.wait_ge(*valued(it, ((tt - 1) % TT, pairs - 1)))
                            for h in range(2):
                                rows = slice(h * window, h * window + window)
                                a = e.tensor_copy(vprev[rows, 1 - tt % 2].rearrange("p (j h) d -> p j h d", h=2)[:, :, h],
                                                  vb[P - window:P, tt % 2].rearrange("p (j h) d -> p j h d", h=2)[:, :, h])
                            a.then_inc(vcarried.sem, 1)
                        elif kind == "out":
                            tile = g.f[:, bass.ds(sequence(step, b) * TT + step[1], 1), :].rearrange("p o c -> p (o c)")
                            if step[1] == 0:
                                e.wait_ge(*xb_ready(it, ("fetch",), 1))
                            e.wait_ge(*ring.written(it, step))
                            e.tensor_tensor(tile, ring.at(step)[:, 0:C], tile, ALU.add).then_inc(ring.empty_of(step), 1)
                        elif kind == "fshift":
                            e.wait_ge(*ring.written(it, ("fturn",), 1))
                            e.wait_ge(*ring.written(it, step))
                            e.tensor_copy(xn[:], ring.at(step).rearrange("p (t c) -> p t c", t=TT)).then_inc(ring.empty_of(step), 1)
                            e.drain()
                            for tt in range(TT):
                                e.bn_stats(stats[:, tt], xn[:, tt])
                            e.drain()
                            for tt in range(TT):
                                e.bn_aggr(mv[:, tt], stats[:, tt])
                            e.drain().then_inc(varied.sem, 1)
                        elif kind == "xn":
                            e.wait_ge(*rstd_ready(it, ("down",)))
                            for tt in range(TT):
                                a = e.tensor_scalar(xn[:, tt], xn[:, tt], mv[:, tt, 0:1],
                                                    rstd[:, tt:tt + 1], ALU.subtract, ALU.mult)
                            a.then_inc(xn_ready.sem, 1)
                        elif kind == "up":
                            c = step[1]
                            n = hid_chunks[c][1]
                            e.wait_ge(*ring.written(it, ("down",), 1))
                            e.wait_ge(*ring.read(it, ("gate", c)))
                            e.wait_ge(*ring.written(it, step))
                            e.scalar_tensor_tensor(hh[0:n, c], ring.at(step)[0:n], b1[0:n, 0, c:c + 1], gate[0:n, c],
                                                   ALU.add, ALU.mult).then_inc(ring.empty_of(step), 1)
                        elif kind == "down":
                            e.wait_ge(*ring.written(it, step))
                            e.tensor_tensor(y[:], ring.at(step).rearrange("p (t c) -> p t c", t=TT), spread(b2[:], 1, TT),
                                            ALU.add).then_inc(ring.empty_of(step), 1)
                            e.drain()
                            x2 = g.f[:, bass.ds(sequence(step, b) * TT, TT), :]
                            e.tensor_tensor(x2, y[:], x2, ALU.add).then_inc(x2_ready.sem, 1)
                            e.drain()
                        elif kind == "end":
                            e.wait_ge(feed_ready, (l + 1) * (16 * FEED_DMAS))
                            e.sem_inc(passed, 1)
                go_round(e, body)

            @block.tensor
            def _(e):
                def body(e, it, b, l, last):
                    for step in STEPS:
                        kind = step[0]
                        if kind in ("shift", "proj", "turn", "oturn", "out", "fshift", "fturn", "gate", "up", "down"):
                            e.wait_ge(*ring.free(it, step))
                            bank, full = ring.at(step), ring.full_of(step)
                        if kind == "shift":
                            if l is None:
                                e.wait_ge(zeroed, 1)
                            e.wait_ge(*xb_ready(it, ("fetch",)))
                            for tt in range(TT):
                                cols = slice(tt * P, tt * P + P)
                                e.matmul(bank[0:DH, cols], xb[:, 1 + tt, 0:DH], g.ident[:], start=True, stop=True)
                                e.matmul(bank[DH:P, cols], xb[:, 1 + tt, DH:C], g.down1[:], start=True, stop=False)
                                a = e.matmul(bank[DH:P, cols], xb[:, tt, DH:C], g.last1[:], start=False, stop=True)
                            a.then_inc(full, 1)
                        elif kind == "proj":
                            _, tt, what, c = step
                            if last and step == early(0)[0]:
                                e.wait_ge(qkv_ready, 32 if l is None else (l + 1) * 32)
                                e.sem_inc(passed, 1)
                            col = "qkv".index(what) * inner + 512 * c
                            e.wait_ge(*ring.read(it, ("shift",), ago(step, ("shift",))))
                            e.matmul(bank[:], hT[:, tt * P:tt * P + P], wqkv[:, col:col + 512],
                                     start=True, stop=True).then_inc(full, 1)
                        elif kind == "turn":
                            _, tt, what, c = step
                            chunk = ("proj",) + step[1:]
                            q = CHUNKS.index(chunk)
                            e.wait_ge(*normed(it, chunk, normed.per * ago(step, chunk)))
                            for j in range(4):
                                a = e.transpose(bank[:, j * P:j * P + P], qn[:, q % QN, 2 * j:2 * j + 2, :], g.ident[:])
                            a.then_inc(full, 1)
                        elif kind == "score":
                            _, tt, j = step
                            s = j % 2
                            if j == 0:
                                needed = [u for u in uses if u[0] in ("proj", "turn") and u[1] == tt]
                                for done in furthest(*[ring.read(it, u, ago(step, u)) for u in needed]):
                                    e.wait_ge(*done)
                                if tt:
                                    before = ("kcarry", tt - 1)
                                    e.wait_ge(*kcarried(it, before, kcarried.per * ago(step, before)))
                            e.wait_ge(*exped(it, (tt, j), 2))
                            e.matmul(s_ps[:, s, 0:2 * keys], g.ident_bf[:], mask[:, min(tt, 1), :], start=True, stop=False)
                            for h in range(2):
                                a = e.matmul(s_ps[:, s, h * keys:(h + 1) * keys], qT[:, tt % 2, h, j, :],
                                             kT[:, tt % 2, j, (1 - h) * window:(1 - h) * window + keys],
                                             start=False, stop=h == 1)
                            a.then_inc(scored.sem, 1)
                        elif kind == "flip":
                            key = step[1:]
                            s = key[1] % 2
                            e.wait_ge(*exped(it, key))
                            e.wait_ge(*unflipped[s](it, key, 1))
                            for h in range(2):
                                own = h * (P + 2 * window)
                                e.transpose(pt_ps[:, s, h], prob[:, s, own:own + P], g.ident[:])
                            a = e.transpose(pt_ps[0:2 * window, s, 2], prob[:, s, P:P + 2 * window], g.ident[:])
                            a.then_inc(flipped.sem, 1)
                        elif kind == "value":
                            _, tt, j = step
                            s = j % 2
                            if j == 0 and tt:
                                before = ("vcarry", tt - 1)
                                e.wait_ge(*vcarried(it, before, vcarried.per * ago(step, before)))
                            e.wait_ge(*unflipped[s](it, (tt, j)))
                            if j % 2 == 0:
                                e.wait_ge(*o_ready(it, (tt, j + 1), 2))
                            for h in range(2):
                                col = (2 * (j % 2) + h) * (DH + 1)
                                out = o_ps[:, (j // 2) % 2, col:col + DH + 1]
                                e.matmul(out, pT[:, s, h], vb[:, tt % 2, 2 * j + h, :], start=True, stop=False)
                                a = e.matmul(out, pTprev[0:2 * window, s], vprev[0:2 * window, tt % 2, 2 * j + h, :],
                                             start=False, stop=True)
                            a.then_inc(valued.sem, 1)
                        elif kind == "oturn":
                            _, tt, u = step
                            e.wait_ge(*o_ready(it, (tt, 4 * u + 3), o_ready.per * lag(step)))
                            for j in range(4):
                                h = 2 * (4 * u + j)
                                a = e.transpose(bank[:, j * P:j * P + P], o_sb[:, h:h + 2, :], g.ident[:])
                            a.then_inc(full, 1)
                        elif kind == "out":
                            tt = step[1]
                            if tt == 0:
                                e.wait_ge(wo_ready, (l + 1) * 16)
                            for done in ring.all_read(it, [("oturn", tt, u) for u in range(pairs // 4)]):
                                e.wait_ge(*done)
                            for j in range(pairs):
                                a = e.matmul(bank[:, 0:C], oT[:, j, :], wo[:, j, :], start=j == 0, stop=j == pairs - 1)
                            a.then_inc(full, 1)
                        elif kind == "fshift":
                            for done in furthest(*[ring.read(it, ("out", tt), ago(step, ("out", tt))) for tt in range(TT)]):
                                e.wait_ge(*done)
                            tile0 = sequence(step, b) * TT
                            x1 = g.f[:, bass.ds(tile0, TT), :]
                            o = bank.rearrange("p (t c) -> p t c", t=TT)
                            e.matmul(o[:, :, 0:DH], g.ident[:], x1[:, :, 0:DH], start=True, stop=True)
                            e.matmul(o[:, :, DH:C], g.down1[:], x1[:, :, DH:C], start=True, stop=False)
                            e.matmul(o[:, 1:TT, DH:C], g.last1[:], g.f[:, bass.ds(tile0, TT - 1), DH:C], start=False,
                                     stop=True).then_inc(full, 1)
                        elif kind == "fturn":
                            e.wait_ge(*xn_ready(it, ("down",)))
                            for tt in range(TT):
                                a = e.transpose(bank[:, tt * P:tt * P + P], xn[:, tt], g.ident[:])
                            a.then_inc(full, 1)
                        elif kind in ("gate", "up"):
                            o, n = hid_chunks[step[1]]
                            if kind == "gate":
                                o += hid
                            e.wait_ge(*ring.read(it, ("fturn",)))
                            e.matmul(bank[0:n, :], w1[:, o:o + n], hnT[:], start=True, stop=True).then_inc(full, 1)
                        elif kind == "down":
                            for done in ring.all_read(it, [("up", c) for c in range(nhc)]):
                                e.wait_ge(*done)
                            for tt in range(TT):
                                for c, (o, n) in enumerate(hid_chunks):
                                    a = e.matmul(bank[:, tt * P:tt * P + P], hh[0:n, c, tt * P:tt * P + P], w2[0:n, c, :],
                                                 start=c == 0, stop=c == nhc - 1)
                            a.then_inc(full, 1)
                        elif kind == "end":
                            e.wait_ge(feed_ready, (l + 1) * (16 * FEED_DMAS))
                            e.sem_inc(passed, 1)
                go_round(e, body)

        for part, steps in (("before", BEFORE), ("main", MAIN), ("after", AFTER)):
            with stage(nc, f"{name}_{part}") as r:
                programs(r, steps)


def mamba_net(nc, g, name, w, center, residual):
    inner, states, rank, taps = 256, 16, 8, 4
    D2 = inner // P
    rows = rank + 2 * states
    INS = [("in", c) for c in range(2 * D2)]
    RING = [("turn",)] + INS + [("dbc",)] + [("dt", d) for d in range(D2)]
    NS = list(range(states))
    ND = [(n, d) for n in NS for d in range(D2)]
    FRONT = [("norm",)] + RING
    BACK = [("state", n) for n in NS] + [("gated",), ("result",)]

    def merged(a, b):
        out, done = [], 0
        for i, s in enumerate(a):
            out.append(s)
            upto = min(len(b), (i + 1) * len(b) // (len(a) - 4))
            out += b[done:upto]
            done = upto
        return out

    with stage(nc, name) as r:
        w_in = r.sb("w_in", [P, 2 * inner])
        w_x = r.sb("w_x", [P, D2, rows])
        w_dt = r.sb("w_dt", [rank, inner])
        w_out = r.sb("w_out", [P, D2, C])
        cols = r.sb("cols", [P, D2, taps + 3])
        ln = r.sb("ln", [P, 2])
        a_log = r.sb("a_log", [P, D2, states])
        decay = r.sb("decay", [P, D2, states])
        half = r.sb("half", [P, TT])
        eps = r.sb("eps", [P, TT])
        sq = r.sb("sq", [P, TT, C])
        stats = r.sb("stats", [P, TT, 6])
        mv = r.sb("mv", [P, TT, 2])
        rstd = r.sb("rstd", [P, TT])
        xn = r.sb("xn", [P, TT, C])
        xnT = r.sb("xnT", [P, SEQ])
        upad = r.sb("upad", [P, D2, taps - 1 + SEQ])
        conv = r.sb("conv", [P, D2, SEQ])
        uc = r.sb("uc", [P, 2, D2, SEQ])
        zs = r.sb("zs", [P, 2, D2, SEQ])
        dbc = r.sb("dbc", [rows, 2, SEQ])
        v = r.sb("v", [P, D2, SEQ])
        ln1 = r.sb("ln1", [P, D2, SEQ])
        delta = r.sb("delta", [P, 2, D2, SEQ])
        du = r.sb("du", [P, 2, D2, SEQ])
        b_sb = r.sb("b_sb", [P, 2, SEQ])
        da = r.sb("da", [P, 4, SEQ])
        dbu = r.sb("dbu", [P, 4, SEQ])
        hid = r.sb("hid", [P, 2, SEQ])
        hc = r.sb("hc", [P, 2, SEQ])
        ty = r.sb("ty", [P, D2, SEQ])
        yz = r.sb("yz", [P, D2, SEQ])
        result = r.sb("result", [P, 2, TT, C])
        ring = r.banks("ring", [r.ps("ring0", [P, 512]), r.ps("ring1", [P, 512])], RING)
        b_ps = r.ps("b", [P, 2, 512])
        c_ps = r.ps("c", [P, 2, 512])
        y_ps = r.ps("y", [P, 2, 512])

        loaded = r.sem("loaded")
        zeroed = r.sem("zeroed")
        decay_ready = r.sem("decay_ready")
        passed = r.sem("passed")
        measured = r.count("measured", ["m"])
        rstd_ready = r.count("rstd_ready", ["r"])
        normed = r.count("normed", ["x"])
        convolved = r.count("convolved", range(D2))
        activated = r.count("activated", range(D2))
        logged = r.count("logged", range(D2))
        stepped = r.count("stepped", range(D2))
        b_full = r.count("b_full", NS)
        b_copied = r.count("b_copied", NS)
        c_full = r.count("c_full", NS)
        da_ready = r.count("da_ready", ND)
        dbu_ready = r.count("dbu_ready", ND)
        scanned = r.count("scanned", ND)
        hc_ready = r.count("hc_ready", ND)
        added = r.count("added", ND)
        yz_ready = r.count("yz_ready", ["y"])
        out_full = r.count("out_full", ["o"])
        stored = r.count("stored", ["s"])
        sent = [r.sem(f"sent{par}") for par in range(2)]
        N_DMA = 8
        block = r.block()

        def sequences(e, front, back):
            def both(b, par):
                for kind, *key in merged(BACK, [("front",) + s for s in FRONT]):
                    if kind == "front":
                        front(b + 1, 1 - par, *key)
                    else:
                        back(b, par, kind, *key)
            for step in FRONT:
                front(0, 0, *step)
            with e.Fori(0, BATCH - 2, 2) as b:
                both(b, 0)
                both(b + 1, 1)
            both(BATCH - 2, 0)
            for step in BACK:
                back(BATCH - 1, 1, *step)

        @block.sync
        def _(e):
            r.give_credit(e)
            for dst, src in ((w_in, "w_in"), (w_x, "w_x"), (w_dt, "w_dt"), (w_out, "w_out"), (cols, "cols"), (ln, "ln"),
                             (a_log, "a_log")):
                e.dma_start(dst[:], w[src]).then_inc(loaded, 16)

            def store(b, par):
                e.wait_ge(*stored(b, "s"))
                e.dma_start(g.s_dram[bass.ds(b, 1)].rearrange("o (t p) c -> p (o t) c", p=P),
                            result[:, par]).then_inc(sent[par], 16)
            for par in range(2):
                e.sem_inc(sent[par], 16)
            with e.Fori(0, BATCH - 1, 2) as b:
                store(b, 0)
                store(b + 1, 1)
            for par in range(2):
                e.wait_ge(sent[par], 16 * (BATCH // 2 + 1))

        @block.gpsimd
        def _(e):
            e.memset(upad[:, :, 0:taps - 1], 0.0)
            e.memset(half[:], -0.5)
            e.memset(eps[:], EPS)
            e.drain().then_inc(zeroed, 1)

            def front(b, par, kind, key=None):
                if kind == "norm":
                    e.wait_ge(*measured(b, "m"))
                    e.tensor_tensor(rstd[:], mv[:, :, 1], eps[:], ALU.add)
                    e.drain()
                    e.tensor_tensor(rstd[:], rstd[:], half[:], ALU.pow).then_inc(rstd_ready.sem, 1)

            def back(b, par, kind, key=None):
                if kind == "state":
                    n = key
                    for d in range(D2):
                        s = (2 * n + d) % 4
                        if d == 0:
                            if n == 0:
                                e.wait_ge(*stepped(b, D2 - 1))
                            e.wait_ge(*b_copied(b, n))
                        e.wait_ge(*scanned(b, (n, d), 4))
                        e.tensor_tensor(dbu[:, s], du[:, par, d], b_sb[:, n % 2], ALU.mult).then_inc(dbu_ready.sem, 1)

            sequences(e, front, back)

        @block.scalar
        def _(e):
            e.wait_ge(loaded, 16 * (N_DMA - 1))
            e.activation(decay[:], a_log[:], ACT.Exp)
            e.drain()
            e.mul(decay[:], decay[:], -1.0)
            e.drain()
            e.wait_ge(zeroed, 1)

            def front(b, par, kind, key=None):
                if kind == "norm":
                    return
                step = (kind,) if key is None else (kind, key)
                bank, empty = ring.at(step), ring.empty_of(step)
                if kind == "turn":
                    e.wait_ge(*ring.written(b, ("in", 2 * D2 - 1), 1))
                    e.wait_ge(*ring.written(b, step))
                    e.activation(xnT[:], bank[:], ACT.Identity, bias=ln[:, 1:2], scale=ln[:, 0:1]).then_inc(empty, 1)
                elif kind == "in" and key < D2:
                    e.wait_ge(*convolved(b, key, D2))
                    e.wait_ge(*ring.written(b, step))
                    e.activation(upad[:, key, taps - 1:], bank[:], ACT.Copy).then_inc(empty, 1)
                elif kind == "in":
                    d = key - D2
                    e.wait_ge(*ring.written(b, step))
                    e.activation(zs[:, par, d], bank[:], ACT.Silu).then_inc(empty, 1)
                    if d == 0:
                        for c in range(D2):
                            e.wait_ge(*convolved(b, c))
                            e.activation(uc[:, par, c], conv[:, c], ACT.Silu,
                                         bias=cols[:, c, taps:taps + 1]).then_inc(activated.sem, 1)
                elif kind == "dbc":
                    e.wait_ge(*ring.written(b, step))
                    e.activation(dbc[:, par], bank[0:rows], ACT.Copy).then_inc(empty, 1)
                elif kind == "dt":
                    d = key
                    e.wait_ge(*stepped(b, d, D2))
                    e.wait_ge(*ring.written(b, step))
                    e.activation(v[:, d], bank[:], ACT.Identity, bias=cols[:, d, taps + 1:taps + 2]).then_inc(empty, 1)
                    e.drain()
                    e.activation(ln1[:, d], v[:, d], ACT.Abs)
                    e.drain()
                    e.activation(ln1[:, d], ln1[:, d], ACT.Exp, scale=-1.0)
                    e.drain()
                    e.activation(ln1[:, d], ln1[:, d], ACT.Ln, bias=1.0).then_inc(logged.sem, 1)

            def back(b, par, kind, key=None):
                if kind != "state":
                    return
                n = key
                if n == 0:
                    e.wait_ge(*stepped(b, D2 - 1))
                e.wait_ge(*dbu_ready(b, (n, 1), 2 * D2))
                e.wait_ge(*b_full(b, n))
                e.activation(b_sb[:, n % 2], b_ps[:, n % 2], ACT.Copy).then_inc(b_copied.sem, 1)
                for d in range(D2):
                    e.wait_ge(*scanned(b, (n, d), 4))
                    e.activation(da[:, (2 * n + d) % 4], delta[:, par, d], ACT.Exp,
                                 scale=decay[:, d, n:n + 1]).then_inc(da_ready.sem, 1)

            sequences(e, front, back)

        @block.vector
        def _(e):
            e.wait_ge(loaded, 16 * (N_DMA - 1))
            e.wait_ge(zeroed, 1)
            e.memset(mv[:, :, 0], 0.0)
            e.drain()

            def front(b, par, kind, key=None):
                x = g.f[:, bass.ds(b * TT, TT), :]
                if kind == "norm":
                    e.wait_ge(*ring.written(b, ("turn",), 1))
                    if center:
                        for tt in range(TT):
                            e.bn_stats(stats[:, tt], g.f[:, bass.ds(b * TT + tt, 1), :].rearrange("p o c -> p (o c)"))
                        e.drain()
                        for tt in range(TT):
                            e.bn_aggr(mv[:, tt], stats[:, tt])
                    else:
                        e.scalar_tensor_tensor(sq[:], x, 1.0 / C, x, ALU.mult, ALU.mult)
                        e.drain()
                        e.tensor_reduce(mv[:, :, 1], sq[:], AX.X, ALU.add)
                    e.drain().then_inc(measured.sem, 1)
                    e.wait_ge(*rstd_ready(b, "r"))
                    for tt in range(TT):
                        o = e.tensor_scalar(xn[:, tt], g.f[:, bass.ds(b * TT + tt, 1), :].rearrange("p o c -> p (o c)"),
                                            mv[:, tt, 0:1], rstd[:, tt:tt + 1], ALU.subtract, ALU.mult)
                    o.then_inc(normed.sem, 1)
                elif kind == "in" and key < D2:
                    d = key
                    e.wait_ge(*ring.read(b, ("in", d)))
                    e.wait_ge(*activated(b, d, D2))
                    tap = lambda k: cols[:, d, k:k + 1]
                    e.tensor_scalar(conv[:, d], upad[:, d, 0:SEQ], tap(0), None, ALU.mult)
                    for k in range(1, taps):
                        e.drain()
                        o = e.scalar_tensor_tensor(conv[:, d], upad[:, d, k:k + SEQ], tap(k), conv[:, d], ALU.mult, ALU.add)
                    o.then_inc(convolved.sem, 1)
                elif kind == "dt":
                    d = key
                    e.wait_ge(*logged(b, d))
                    e.scalar_tensor_tensor(delta[:, par, d], v[:, d], 0.0, ln1[:, d], ALU.max, ALU.add)
                    e.drain()
                    e.tensor_tensor(du[:, par, d], delta[:, par, d], uc[:, par, d], ALU.mult).then_inc(stepped.sem, 1)

            def back(b, par, kind, key=None):
                if kind == "state":
                    n = key
                    for d in range(D2):
                        s = (2 * n + d) % 4
                        e.wait_ge(*da_ready(b, (n, d)))
                        e.wait_ge(*dbu_ready(b, (n, d)))
                        e.tensor_tensor_scan(hid[:, d], da[:, s], dbu[:, s], 0.0, ALU.mult, ALU.add).then_inc(scanned.sem, 1)
                        e.wait_ge(*scanned(b, (n, d)))
                        if d == 0:
                            e.wait_ge(*c_full(b, n))
                        e.wait_ge(*added(b, (n, d), 2))
                        e.tensor_tensor(hc[:, d], hid[:, d], c_ps[:, n % 2], ALU.mult).then_inc(hc_ready.sem, 1)
                elif kind == "gated":
                    e.wait_ge(*added(b, ND[-1]))
                    for d in range(D2):
                        e.scalar_tensor_tensor(ty[:, d], uc[:, par, d], cols[:, d, taps + 2:taps + 3], y_ps[:, d],
                                               ALU.mult, ALU.add)
                    e.drain()
                    e.wait_ge(*out_full(b, "o", 1))
                    e.tensor_tensor(yz[:], ty[:], zs[:, par], ALU.mult).then_inc(yz_ready.sem, 1)
                elif kind == "result":
                    e.wait_ge(*out_full(b, "o"))
                    dst, x = result[:, par], g.f[:, bass.ds(b * TT, TT), :]
                    e.wait_ge(sent[par], (b - par) * 8 + 16)
                    o = y_ps[:, 0].rearrange("p (t c) -> p t c", t=TT)
                    if residual:
                        e.tensor_tensor(dst, o, x, ALU.add).then_inc(stored.sem, 1)
                    else:
                        e.tensor_copy(dst, o).then_inc(stored.sem, 1)

            sequences(e, front, back)

        @block.tensor
        def _(e):
            e.wait_ge(loaded, 16 * (N_DMA - 1))

            def front(b, par, kind, key=None):
                if kind == "norm":
                    return
                step = (kind,) if key is None else (kind, key)
                bank, full = ring.at(step), ring.full_of(step)
                e.wait_ge(*ring.free(b, step))
                if kind == "turn":
                    e.wait_ge(*normed(b, "x"))
                    for tt in range(TT):
                        o = e.transpose(bank[:, tt * P:tt * P + P], xn[:, tt], g.ident[:])
                    o.then_inc(full, 1)
                elif kind == "in":
                    e.wait_ge(*ring.read(b, ("turn",)))
                    e.matmul(bank[:], w_in[:, key * P:key * P + P], xnT[:], start=True, stop=True).then_inc(full, 1)
                elif kind == "dbc":
                    e.wait_ge(*activated(b, D2 - 1))
                    for d in range(D2):
                        o = e.matmul(bank[0:rows], w_x[:, d, :], uc[:, par, d], start=d == 0, stop=d == D2 - 1)
                    o.then_inc(full, 1)
                elif kind == "dt":
                    e.wait_ge(*ring.read(b, ("dbc",)))
                    e.matmul(bank[:], w_dt[:, key * P:key * P + P], dbc[0:rank, par], start=True, stop=True).then_inc(full, 1)

            def back(b, par, kind, key=None):
                def add(n):
                    for d in range(D2):
                        e.wait_ge(*hc_ready(b, (n, d)))
                        if (n, d) == (0, 0):
                            e.wait_ge(*stored(b, "s", 1))
                        e.matmul(y_ps[:, d], g.ident[:], hc[:, d], start=n == 0, stop=n == states - 1).then_inc(added.sem, 1)

                def row(i):
                    return g.ident[0:rows, i:i + 1].broadcast_to([rows, P])

                if kind == "state":
                    n = key
                    if n == 0:
                        e.wait_ge(*ring.read(b, ("dbc",)))
                    e.wait_ge(*b_copied(b, n, 2))
                    e.matmul(b_ps[:, n % 2], row(rank + n), dbc[:, par], start=True, stop=True).then_inc(b_full.sem, 1)
                    e.wait_ge(*hc_ready(b, (n, 1), 4))
                    e.matmul(c_ps[:, n % 2], row(rank + states + n), dbc[:, par], start=True, stop=True).then_inc(c_full.sem, 1)
                    if n:
                        add(n - 1)
                elif kind == "gated":
                    add(states - 1)
                elif kind == "result":
                    e.wait_ge(*yz_ready(b, "y"))
                    for tt in range(TT):
                        for d in range(D2):
                            o = e.matmul(y_ps[:, 0, tt * C:tt * C + C], yz[:, d, tt * P:tt * P + P], w_out[:, d, :],
                                         start=d == 0, stop=d == D2 - 1)
                    o.then_inc(out_full.sem, 1)

            sequences(e, front, back)


def ttt_net(nc, g, name, w):
    H, CH = 16, 64
    HP, NCHUNK, SP2 = H // 2, SEQ // CH, BATCH // 2
    LR_BASE, WD_BASE = 0.001, 0.9
    with ExitStack() as shared:
        sb = lambda n, shape: shared.enter_context(nc.sbuf_tensor(f"{name}_{n}", shape, F32))
        xT = sb("xT", [P, BATCH, SEQ])
        rates = sb("rates", [P, NCHUNK, SP2, 2 * H])
        decays = sb("decays", [P, 2, HP, BATCH, NCHUNK])

        with stage(nc, name + "p") as r:
            w_rates = r.sb("w_rates", [P, 4 * H])
            base = r.sb("base", [4 * H, 1])
            gates = r.sb("gates", [4 * H, 2, SEQ])
            mean = r.sb("mean", [4 * H, BATCH, NCHUNK])
            rows = r.sb("rows", [4 * H, 2 * H, 64])
            wide = r.sb("wide", [4 * H, NCHUNK, BATCH, CH])
            t_ps = [r.ps(f"t{i}", [P, 512]) for i in range(2)]
            r_ps = [r.ps(f"r{i}", [P, 512]) for i in range(2)]
            a_ps = [r.ps(f"a{i}", [P, 8, 64]) for i in range(2)]
            b_ps = [r.ps(f"b{i}", [P, 16, 2 * H]) for i in range(2)]
            loaded = r.sem("loaded")
            turned = r.sem("turned")
            copied = r.sem("copied")
            rated = r.sem("rated")
            gated = r.sem("gated")
            summed = r.sem("summed")
            mean_ready = r.sem("mean_ready")
            spread_out = r.sem("spread_out")
            block = r.block()

            @block.sync
            def _(e):
                e.dma_start(w_rates[:], w["w_rates"]).then_inc(loaded, 16)
                e.dma_start(base[:], w["base"]).then_inc(loaded, 16)
                e.wait_ge(loaded, 32)

            @block.tensor
            def _(e):
                e.wait_ge(loaded, 32)
                for b in range(BATCH):
                    if b >= 2:
                        e.wait_ge(copied, b - 1)
                    for tt in range(TT):
                        o = e.transpose(t_ps[b % 2][:, tt * P:tt * P + P], g.f[:, b * TT + tt, :], g.ident[:])
                    o.then_inc(turned, 1)
                for b in range(BATCH):
                    e.wait_ge(copied, b + 1)
                    if b >= 2:
                        e.wait_ge(gated, b - 1)
                    e.matmul(r_ps[b % 2][0:4 * H, :], w_rates[:], xT[:, b, :], start=True, stop=True).then_inc(rated, 1)
                e.wait_ge(mean_ready, 1)
                for k in range(2):
                    for p in range(HP):
                        r0 = 2 * H + k * H + 2 * p
                        lhs = rows[:, r0 - 2 * H:r0 - 2 * H + 2, :]
                        e.matmul(a_ps[k][:, p, :], lhs, mean[:], start=True, stop=True)
                for c in range(NCHUNK):
                    for sp in range(SP2):
                        lhs = wide[:, c, 2 * sp:2 * sp + 2, :]
                        o = e.matmul(b_ps[c // 4][:, (c % 4) * SP2 + sp, :], lhs, g.ident[0:4 * H, 0:2 * H],
                                     start=True, stop=True)
                o.then_inc(spread_out, 1)

            @block.scalar
            def _(e):
                for b in range(BATCH):
                    e.wait_ge(turned, b + 1)
                    e.activation(xT[:, b, :], t_ps[b % 2][:], ACT.Copy).then_inc(copied, 1)
                for b in range(BATCH):
                    e.wait_ge(rated, b + 1)
                    if b >= 2:
                        e.wait_ge(summed, b - 1)
                    e.activation(gates[:, b % 2], r_ps[b % 2][0:4 * H, :], ACT.Sigmoid).then_inc(gated, 1)

            @block.vector
            def _(e):
                for b in range(BATCH):
                    e.wait_ge(gated, b + 1)
                    e.tensor_reduce(mean[:, b, :], gates[:, b % 2].rearrange("p (c n) -> p c n", n=CH), AX.X,
                                    ALU.add).then_inc(summed, 1)
                e.wait_ge(summed, BATCH)
                e.tensor_scalar(mean[:], mean[:], base[:, 0:1], None, ALU.mult)
                e.drain()
                e.tensor_copy(rows[:], spread(g.ident[0:4 * H, 2 * H:4 * H], 2, 64))
                for c in range(NCHUNK):
                    e.tensor_copy(wide[:, c], spread(mean[:, :, c], 2, CH))
                e.drain().then_inc(mean_ready, 1)
                e.wait_ge(spread_out, 1)
                for k in range(2):
                    e.tensor_copy(decays[:, k], a_ps[k].rearrange("p q (b c) -> p q b c", b=BATCH))
                    e.tensor_copy(rates[:, 4 * k:4 * k + 4],
                                  b_ps[k].rearrange("p (c s) r -> p c s r", c=4))

        F = [(what, j) for what in ("qT", "kT", "vT", "kn", "vn") for j in range(2)]
        Z = [(what, j) for what in ("zq", "zk") for j in range(2)]
        B = [(what, j) for what in ("pn", "oT", "a", "gout", "goutT", "gin") for j in range(2)] + [("out", 0)]
        STEP = range(SP2)
        keys = [(0, k) for k in F + Z] + [(SP2 - 1, k) for k in B]
        for i in range(1, SP2):
            keys += [(i, k) for k in F + Z] + [(i - 1, k) for k in B]
        with stage(nc, name) as r:
            wq = r.sb("wq", [P, H * 64])
            wk = r.sb("wk", [P, H * 64])
            wv = r.sb("wv", [P, H * 64])
            wo = r.sb("wo", [P, HP, C])
            win_t = r.sb("win_t", [P, BATCH, HP, 64])
            wout = r.sb("wout", [P, BATCH, HP, 64])
            wout_t = r.sb("wout_t", [P, BATCH, HP, 64])
            xc = r.sb("xc", [P, 2, 2, CH])
            qT = r.sb("qT", [P, 2, HP, 2, CH])
            kT = r.sb("kT", [P, 2, HP, 2, CH])
            vT = r.sb("vT", [P, 2, HP, 2, CH])
            kn = r.sb("kn", [P, 2, H, 64])
            vn = r.sb("vn", [P, 2, H, 64])
            top = r.sb("top", [P, 2, 2, 8])
            zq = r.sb("zq", [P, 2, HP, 2, CH])
            zk = r.sb("zk", [P, 2, HP, 2, CH])
            total = r.sb("total", [P, 2, 2, 16])
            pn = r.sb("pn", [P, HP, 2, 64])
            oT = r.sb("oT", [P, HP, 2 * CH])
            pa = r.sb("pa", [P, 2, HP, 64])
            sums = r.sb("sums", [P, 2, HP])
            gz = r.sb("gz", [P, HP, 2, 64])
            ost = r.sb("ost", [P, 2, C])
            NB = 6
            ring = r.banks("ring", [r.ps(f"ring{i}", [P, 512]) for i in range(NB)], keys)
            loaded = r.sem("loaded")
            xc_ready = r.count("xc_ready", STEP)
            kn_ready = r.count("kn_ready", STEP)
            exped = r.count("exped", [(i, q) for i in STEP for q in "qk"])
            rq_ready = r.count("rq_ready", STEP)
            pq_ready = r.count("pq_ready", STEP)
            pk_ready = r.count("pk_ready", STEP)
            a_ready = r.count("a_ready", STEP)
            gz_ready = r.count("gz_ready", STEP)
            decayed = {m: r.count(f"decayed_{m}", STEP) for m in ("wout", "wout_t", "win_t")}
            passed_pe = r.sem("passed_pe")
            passed = r.sem("passed")
            stored = [r.sem(f"stored{k}") for k in range(2)]
            block = r.block()

            def wait(e, need):
                for w in furthest(*need):
                    e.wait_ge(*w)
                need.clear()

            def pass_by(e, c, step_keys):
                if e is not nc.tensor:
                    return
                for key in step_keys:
                    e.wait_ge(*ring.free(c, key))
                    e.sem_inc(ring.full_of(key), 1)
                    e.sem_inc(ring.empty_of(key), 1)

            def steps(e, front, back):
                for k in F + Z:
                    front(0, 0, k)
                pass_by(e, 0, [(SP2 - 1, k) for k in B])

                def chunk(c, last):
                    for i in STEP:
                        if not (last and i == SP2 - 1):
                            for k in F + Z:
                                front(c + (i + 1) // SP2, (i + 1) % SP2, k)
                        else:
                            pass_by(e, c + 1, [(0, k) for k in F + Z])
                        for k in B:
                            back(c, i, k)
                with e.Fori(0, NCHUNK - 1) as c:
                    chunk(c, False)
                chunk(NCHUNK - 1, True)

            def period(i, k, back):
                j = i - back
                key = (j % SP2, k)
                return key, j // SP2 + (1 if key[0] == SP2 - 1 and k in B else 0)

            def wrt(c, i, k, back=0):
                key, ahead = period(i, k, back)
                return ring.written(c, key, -ahead)

            def red(c, i, k, back=0):
                key, ahead = period(i, k, back)
                return ring.read(c, key, -ahead)

            def free(c, i, k):
                key, ahead = period(i, k, 0)
                empty = ring.empty[ring.where[key]]
                return empty(c, key, 1 - ahead * empty.per)

            @block.sync
            def _(e):
                r.give_credit(e)
                for q in stored:
                    e.sem_inc(q, 32)
                for dst, src in ((wq, "wq"), (wk, "wk"), (wv, "wv"), (wo, "wo")):
                    e.dma_start(dst[:], w[src]).then_inc(loaded, 16)
                for dst, src in ((win_t, "win_t"), (wout, "wout"), (wout_t, "wout_t")):
                    for b in range(BATCH):
                        e.dma_start(dst[:, b], w[src]).then_inc(loaded, 16)

                def store(c, i):
                    e.wait_ge(*red(c, i, ("out", 0)))
                    for s in range(2):
                        dst = g.s_dram[2 * i + s, bass.ds(c * CH, CH), :]
                        e.dma_start(dst, ost[s * CH:s * CH + CH, i % 2]).then_inc(stored[i % 2], 16)
                with e.Fori(0, NCHUNK) as c:
                    for i in STEP:
                        store(c, i)
                for k in range(2):
                    e.wait_ge(stored[k], 32 + 32 * (SP2 // 2) * NCHUNK)

            LOADED = 16 * (4 + 3 * BATCH)

            @block.gpsimd
            def _(e):
                e.wait_ge(loaded, LOADED)

                def front(c, i, k):
                    need = []
                    par = i % 2
                    if k == ("qT", 0):
                        need.append(wrt(c, i, ("vn", 1), 2))
                        need.append(wrt(c, i, ("vn", 0), 2))
                        wait(e, need)
                        e.sem_inc(passed, 1)
                        e.tensor_copy(xc[:, par], xT[:, 2 * i:2 * i + 2, bass.ds(c * CH, CH)]).then_inc(xc_ready.sem, 1)
                    elif k == ("kn", 1):
                        for j in range(2):
                            need.append(red(c, i, ("kn", j)))
                        wait(e, need)
                        e.sem_inc(passed, 1)
                        rate = rates[:, bass.ds(c, 1), i, 0:H].rearrange("p o h -> p (o h)")
                        e.tensor_tensor(kn[:, par], kn[:, par], spread(rate, 2, 64), ALU.mult).then_inc(kn_ready.sem, 1)
                    elif k == ("zq", 1):
                        need.append(rq_ready(c, i))
                        z = zq[:, par].rearrange("p q s n -> p (q s) n")
                        wait(e, need)
                        e.tensor_tensor(z, z, spread(total[:, par, 0], 2, CH), ALU.mult).then_inc(pq_ready.sem, 1)

                def back(c, i, k):
                    need = []
                    mats = {("gout", 0): ("wout", wout, 1, ("oT", 1)), ("goutT", 0): ("wout_t", wout_t, 1, ("a", 1)),
                            ("pn", 0): ("win_t", win_t, 0, ("zk", 1))}
                    if k in mats:
                        what, mat, kind, reader = mats[k]
                        need.append(wrt(c, i, reader))
                        need.append(wrt(c, i, (reader[0], 0)))
                        wait(e, need)
                        e.sem_inc(passed, 1)
                        rate = decays[:, kind, :, 2 * i:2 * i + 2, bass.ds(c, 1)].rearrange("p q s o -> p s (q o)")
                        m = mat[:, 2 * i:2 * i + 2]
                        e.tensor_tensor(m, m, spread(rate, 3, 64), ALU.mult).then_inc(decayed[what].sem, 1)
                    elif k == ("a", 1):
                        need.append(a_ready(c, i))
                        need.append(wrt(c, i, ("gin", 1), 1))
                        need.append(wrt(c, i, ("gin", 0), 1))
                        for h in range(2):
                            wait(e, need)
                            o = e.tensor_tensor(gz[:, :, h], pn[:, :, h], pa[:, h], ALU.mult)
                        o.then_inc(gz_ready.sem, 1)

                steps(e, front, back)

            @block.scalar
            def _(e):
                e.wait_ge(loaded, LOADED)

                def front(c, i, k):
                    need = []
                    what, j = k
                    par = i % 2
                    if what in ("zq", "zk"):
                        if j == 0:
                            return
                        z = zq if what == "zq" else zk
                        for jj in range(2):
                            need.append(red(c, i, (what, jj)))
                        wait(e, need)
                        e.activation(z[:, par], z[:, par], ACT.Exp).then_inc(exped.sem, 1)
                        return
                    if what == "vn":
                        return
                    dst, reader, n = {"qT": (qT, "zq", 2), "kT": (kT, "zk", 2), "vT": (vT, "a", 2), "kn": (kn, "gin", 2)}[what]
                    if j == 0:
                        need.append(wrt(c, i, (reader, 0), 2))
                        need.append(wrt(c, i, (reader, 1), 2))
                    need.append(wrt(c, i, k))
                    if what == "kn":
                        d = kn[:, par, 8 * j:8 * j + 8]
                        src = ring.at((i, k)).rearrange("p (h d) -> p h d", h=8)
                    else:
                        d = dst[:, par, 4 * j:4 * j + 4]
                        src = ring.at((i, k)).rearrange("p (q s n) -> p q s n", q=4, s=2)
                    wait(e, need)
                    e.activation(d, src, ACT.Copy if what == "vT" else ACT.Silu).then_inc(ring.empty_of((i, k)), 1)

                def back(c, i, k):
                    need = []
                    what, j = k
                    if what == "pn":
                        if j == 0:
                            need.append(gz_ready(c, i, 1))
                            need.append(wrt(c, i, ("goutT", 0), 1))
                            need.append(wrt(c, i, ("goutT", 1), 1))
                        need.append(wrt(c, i, k))
                        wait(e, need)
                        e.activation(pn[:, 4 * j:4 * j + 4], ring.at((i, k)).rearrange("p (q h d) -> p q h d", q=4, h=2),
                                     ACT.Copy).then_inc(ring.empty_of((i, k)), 1)
                    elif what == "oT":
                        if j == 0:
                            need.append(wrt(c, i, ("out", 0), 1))
                        need.append(wrt(c, i, k))
                        wait(e, need)
                        e.activation(oT[:, 4 * j:4 * j + 4], ring.at((i, k)).rearrange("p (q n) -> p q n", q=4),
                                     ACT.Copy).then_inc(ring.empty_of((i, k)), 1)
                    elif what == "out":
                        e.wait_ge(stored[i % 2], 32 * (c * (SP2 // 2) + i // 2) + 32)
                        need.append(wrt(c, i, k))
                        wait(e, need)
                        e.activation(ost[:, i % 2], ring.at((i, k))[:, 0:C], ACT.Copy).then_inc(ring.empty_of((i, k)), 1)

                steps(e, front, back)

            @block.vector
            def _(e):
                e.wait_ge(loaded, LOADED)

                def front(c, i, k):
                    need = []
                    what, j = k
                    par = i % 2
                    if what == "vn":
                        if j == 0:
                            need.append(wrt(c, i, ("goutT", 0), 2))
                            need.append(wrt(c, i, ("goutT", 1), 2))
                        need.append(wrt(c, i, k))
                        rate = rates[:, bass.ds(c, 1), i, H + 8 * j:H + 8 * j + 8].rearrange("p o h -> p (o h)")
                        wait(e, need)
                        e.tensor_tensor(vn[:, par, 8 * j:8 * j + 8], ring.at((i, k)).rearrange("p (h d) -> p h d", h=8),
                                        spread(rate, 2, 64), ALU.mult).then_inc(ring.empty_of((i, k)), 1)
                    elif what in ("zq", "zk"):
                        q = what == "zq"
                        z = zq if q else zk
                        if j == 0:
                            reader = "oT" if q else "pn"
                            need.append(wrt(c, i, (reader, 0), 2))
                            need.append(wrt(c, i, (reader, 1), 2))
                        need.append(wrt(c, i, k))
                        src = ring.at((i, k)).rearrange("p (u n) -> p u n", u=8)
                        t = top[:, 0 if q else 1, j]
                        wait(e, need)
                        e.tensor_reduce(t, src, AX.X, ALU.max)
                        e.drain()
                        e.tensor_tensor(z[:, par, 4 * j:4 * j + 4].rearrange("p q s n -> p (q s) n"), src, spread(t, 2, CH),
                                        ALU.subtract).then_inc(ring.empty_of((i, k)), 1)
                        if k == ("zk", 1):
                            for n, (what, z) in enumerate((("q", zq), ("k", zk))):
                                need.append(exped(c, (i, what)))
                                z = z[:, par].rearrange("p q s n -> p (q s) n")
                                wait(e, need)
                                e.tensor_reduce(total[:, par, n], z, AX.X, ALU.add)
                                e.drain()
                                o = e.reciprocal(total[:, par, n], total[:, par, n])
                                if what == "q":
                                    o.then_inc(rq_ready.sem, 1)
                                else:
                                    e.drain()
                                    e.tensor_tensor(z, z, spread(total[:, par, n], 2, CH), ALU.mult).then_inc(pk_ready.sem, 1)

                def back(c, i, k):
                    need = []
                    what, j = k
                    if what == "a":
                        if j == 0:
                            for jj in range(2):
                                need.append(red(c, i, ("pn", jj)))
                            need.append(gz_ready(c, i, 1))
                        need.append(wrt(c, i, k))
                        src = ring.at((i, k)).rearrange("p (q d) -> p q d", q=HP)
                        wait(e, need)
                        e.tensor_tensor(pa[:, j], src, pn[:, :, j], ALU.mult)
                        e.drain()
                        e.tensor_reduce(sums[:, j], pa[:, j], AX.X, ALU.add)
                        e.drain()
                        e.tensor_tensor(pa[:, j], src, spread(sums[:, j], 2, 64), ALU.subtract).then_inc(ring.empty_of((i, k)), 1)
                        if j:
                            e.drain().then_inc(a_ready.sem, 1)
                    elif what in ("gout", "goutT", "gin"):
                        name_, mat = {"gout": ("wout", wout), "goutT": ("wout_t", wout_t), "gin": ("win_t", win_t)}[what]
                        need.append(decayed[name_](c, i))
                        need.append(wrt(c, i, k))
                        m = mat[:, 2 * i + j]
                        wait(e, need)
                        e.tensor_tensor(m, m, ring.at((i, k)).rearrange("p (q d) -> p q d", q=HP),
                                        ALU.add).then_inc(ring.empty_of((i, k)), 1)

                steps(e, front, back)

            @block.tensor
            def _(e):
                e.wait_ge(loaded, LOADED)
                half = lambda h: slice(64 * h, 64 * h + 64)

                def wait_here(need):
                    wait(e, need)
                    e.sem_inc(passed_pe, 1)

                def front(c, i, k):
                    what, j = k
                    par = i % 2
                    bank, full = ring.at((i, k)), ring.full_of((i, k))
                    need = [free(c, i, k)]
                    if what in ("qT", "kT", "vT"):
                        need.append(xc_ready(c, i))
                        wt = {"qT": wq, "kT": wk, "vT": wv}[what]
                        wait_here(need)
                        for q in range(4):
                            col = (4 * j + q) * P
                            o = e.matmul(bank[:, q * P:q * P + P], wt[:, col:col + P], xc[:, par], start=True, stop=True)
                    elif what in ("kn", "vn"):
                        wt = wk if what == "kn" else wv
                        wait_here(need)
                        o = e.matmul(bank[:], xc[:, par], wt[:, 512 * j:512 * j + 512], start=True, stop=True)
                    else:
                        src, proj = (qT, "qT") if what == "zq" else (kT, "kT")
                        for jj in range(2):
                            need.append(red(c, i, (proj, jj)))
                        if k == ("zq", 0):
                            need.append(red(c, i, ("gin", 0), SP2))
                            need.append(red(c, i, ("gin", 1), SP2))
                        wait_here(need)
                        for q in range(4):
                            p = 4 * j + q
                            for s in range(2):
                                for h in range(2):
                                    o = e.matmul(bank[half(h), (2 * q + s) * CH:(2 * q + s + 1) * CH],
                                                 win_t[half(h), 2 * i + s, p, :], src[half(h), par, p, s, :],
                                                 start=True, stop=True)
                    o.then_inc(full, 1)

                def back(c, i, k):
                    what, j = k
                    par = i % 2
                    bank, full = ring.at((i, k)), ring.full_of((i, k))
                    need = [free(c, i, k)]
                    if what == "pn":
                        need.append(pk_ready(c, i))
                        wait_here(need)
                        for q in range(4):
                            o = e.transpose(bank[:, q * P:q * P + P], zk[:, par, 4 * j + q], g.ident[:])
                    elif what == "oT":
                        need.append(pq_ready(c, i))
                        if j == 0:
                            for jj in range(2):
                                need.append(red(c, i, ("gout", jj), SP2))
                        wait_here(need)
                        for q in range(4):
                            p = 4 * j + q
                            for s in range(2):
                                for h in range(2):
                                    o = e.matmul(bank[half(h), (2 * q + s) * CH:(2 * q + s + 1) * CH],
                                                 wout[half(h), 2 * i + s, p, :], zq[half(h), par, p, s, :],
                                                 start=True, stop=True)
                    elif what == "a":
                        if j == 0:
                            for jj in range(2):
                                need.append(red(c, i, ("vT", jj)))
                                need.append(red(c, i, ("goutT", jj), SP2))
                        wait_here(need)
                        for p in range(HP):
                            for s in range(2):
                                o = e.matmul(bank[half(s), p * 64:p * 64 + 64], vT[half(j), par, p, s, :],
                                             wout_t[half(j), 2 * i + s, p, :], start=True, stop=True)
                    elif what in ("gout", "goutT", "gin"):
                        if j == 0:
                            for jj in range(2):
                                need.append(red(c, i, ("pn", jj)))
                                need.append(red(c, i, ("vn", jj)))
                            if what == "gin":
                                need.append(gz_ready(c, i))
                                need.append(kn_ready(c, i))
                        wait_here(need)
                        for p in range(HP):
                            for h in range(2):
                                pp, vv = pn[half(j), p, h, :], vn[half(j), par, 2 * p + h, :]
                                lhs, rhs = {"gout": (pp, vv), "goutT": (vv, pp),
                                            "gin": (kn[half(j), par, 2 * p + h, :], gz[half(j), p, h, :])}[what]
                                o = e.matmul(bank[half(h), p * 64:p * 64 + 64], lhs, rhs, start=True, stop=True)
                    elif what == "out":
                        for jj in range(2):
                            need.append(red(c, i, ("oT", jj)))
                        wait_here(need)
                        for p in range(HP):
                            o = e.matmul(bank[:, 0:C], oT[:, p, :], wo[:, p, :], start=p == 0, stop=p == HP - 1)
                    o.then_inc(full, 1)

                steps(e, front, back)


def moe_net(nc, g, name, w):
    E, I, G, TG, K, CAP, SCALE = 64, 64, 8, 4, 8, 64, 2.5
    EG, NP = E // G, E // 2
    RING = [("turn",), ("logits",), ("pos",), ("wturn",)]
    for j in range(NP):
        RING += [("g", j), ("u", j), ("w", j)]
    RING += [("g", NP), ("u", NP)]
    NB = 6
    with stage(nc, name) as r:
        router = r.sb("router", [P, E])
        wg = r.sb("wg", [P, NP, P])
        wu = r.sb("wu", [P, NP, P])
        wd = r.sb("wd", [P, NP, C])
        sg = r.sb("sg", [P, I])
        su = r.sb("su", [P, I])
        sd = r.sb("sd", [I, C])
        pick = r.sb("pick", [E, E, I])
        fb = r.sb("fb", [P, TT, C])
        xT = r.sb("xT", [P, SEQ])
        score = r.sb("score", [P, TT, E])
        groups = r.sb("groups", [P, TT, 16])
        best = r.sb("best", [P, TT, 8])
        out_groups = r.sb("out_groups", [P, TT, 8])
        rest = r.sb("rest", [P, TT, 16])
        gmask = r.sb("gmask", [P, TT, G])
        masked = r.sb("masked", [P, TT, E])
        top = r.sb("top", [P, TT, 8])
        left = r.sb("left", [P, TT, E])
        sel = r.sb("sel", [P, TT, E])
        den = r.sb("den", [P, TT])
        wt = r.sb("wt", [P, TT, E])
        taken = r.sb("taken", [P, E])
        now = r.sb("now", [P, E])
        wT = r.sb("wT", [E, SEQ])
        sil = r.sb("sil", [P, 2, SEQ])
        hh = r.sb("hh", [P, 2, SEQ])
        h2 = r.sb("h2", [P, 2, SEQ])
        ring = r.banks("ring", [r.ps(f"ring{i}", [P, 512]) for i in range(NB)], RING)
        acc = r.ps("acc", [P, 512])
        JS = list(range(NP + 1))
        loaded = r.sem("loaded")
        zeroed = r.sem("zeroed")
        passed = r.sem("passed")
        fb_ready = r.count("fb_ready", ["fb"])
        chosen = r.count("chosen", ["sel"])
        weighed = r.count("weighed", ["w"])
        silued = r.count("silued", JS)
        h_ready = r.count("h_ready", JS)
        down = r.count("down", JS)
        stored = r.count("stored", ["f"])
        N_DMA = 16 * 7
        block = r.block()

        @block.sync
        def _(e):
            r.give_credit(e)
            for dst, src in ((router, "router"), (wg, "wg"), (wu, "wu"), (wd, "wd"), (sg, "sg"), (su, "su"), (sd, "sd")):
                e.dma_start(dst[:], w[src]).then_inc(loaded, 16)
            e.wait_ge(loaded, N_DMA)

        @block.gpsimd
        def _(e):
            e.memset(groups[:], -1.0)
            e.memset(out_groups[:], -1.0)
            e.memset(taken[:], 0.0)
            e.drain().then_inc(zeroed, 1)
            with e.Fori(0, BATCH) as b:
                e.wait_ge(*ring.written(b, ("turn",), 1))
                e.sem_inc(passed, 1)
                e.tensor_copy(fb[:], g.f[:, bass.ds(b * TT, TT), :]).then_inc(fb_ready.sem, 1)

        @block.scalar
        def _(e):
            with e.Fori(0, BATCH) as b:
                for step in RING:
                    kind = step[0]
                    bank, empty = ring.at(step), ring.empty_of(step)
                    if kind == "turn":
                        e.wait_ge(*ring.written(b, ("u", NP), 1))
                        e.wait_ge(*ring.written(b, step))
                        e.activation(xT[:], bank[:], ACT.Copy).then_inc(empty, 1)
                    elif kind == "logits":
                        e.wait_ge(*chosen(b, "sel", 1))
                        e.wait_ge(*ring.written(b, step))
                        e.activation(score[:], bank[:, 0:TT * E].rearrange("p (t c) -> p t c", t=TT),
                                     ACT.Sigmoid).then_inc(empty, 1)
                    elif kind == "wturn":
                        e.wait_ge(*ring.written(b, ("w", NP - 1), 1))
                        e.wait_ge(*ring.written(b, step))
                        e.activation(wT[:], bank[0:E], ACT.Copy).then_inc(empty, 1)
                    elif kind == "g":
                        j = step[1]
                        n = P if j < NP else I
                        e.wait_ge(*h_ready(b, j, 2))
                        e.wait_ge(*ring.written(b, step))
                        e.activation(sil[0:n, j % 2], bank[0:n], ACT.Silu).then_inc(empty, 1)

        @block.vector
        def _(e):
            e.wait_ge(zeroed, 1)
            e.tensor_copy(pick[:], spread(g.ident[0:E, 0:E], 2, I))
            e.drain()
            with e.Fori(0, BATCH) as b:
                for step in RING:
                    kind = step[0]
                    bank, empty = ring.at(step), ring.empty_of(step)
                    if kind == "logits":
                        e.wait_ge(*ring.read(b, step))
                        e.tensor_reduce(groups[:, :, 0:G], score.rearrange("p t (g k) -> p t g k", g=G), AX.X, ALU.max)
                        e.drain()
                        for tt in range(TT):
                            e.max(best[:, tt], groups[:, tt, 0:G])
                        e.drain()
                        e.tensor_copy(out_groups[:, :, 0:TG], best[:, :, 0:TG])
                        e.drain()
                        for tt in range(TT):
                            e.match_replace(rest[:, tt], out_groups[:, tt], groups[:, tt], -2.0)
                        e.drain()
                        e.tensor_scalar(gmask[:], rest[:, :, 0:G], -1.5, None, ALU.is_lt)
                        e.drain()
                        e.tensor_tensor(masked.rearrange("p t (g k) -> p (t g) k", g=G),
                                        score.rearrange("p t (g k) -> p (t g) k", g=G),
                                        spread(gmask.rearrange("p t g -> p (t g)"), 2, EG), ALU.mult)
                        e.drain()
                        for tt in range(TT):
                            e.max(top[:, tt], masked[:, tt])
                        e.drain()
                        for tt in range(TT):
                            e.match_replace(left[:, tt], top[:, tt], masked[:, tt], -1.0)
                        e.tensor_reduce(den[:], top[:], AX.X, ALU.add)
                        e.drain()
                        e.tensor_scalar(sel[:], left[:], -0.5, None, ALU.is_lt)
                        e.tensor_scalar(den[:], den[:], 1e-9, None, ALU.max)
                        e.drain()
                        e.reciprocal(den[:], den[:])
                        e.scalar_tensor_tensor(wt[:], sel[:], SCALE, masked[:], ALU.mult, ALU.mult)
                        e.drain()
                        e.tensor_tensor(wt[:], wt[:], spread(den[:], 2, E), ALU.mult).then_inc(chosen.sem, 1)
                        e.drain()
                    elif kind == "pos":
                        e.wait_ge(*ring.written(b, step))
                        e.scalar_tensor_tensor(wt[:], bank[:, 0:TT * E].rearrange("p (t c) -> p t c", t=TT), CAP - 0.5, wt[:],
                                               ALU.is_lt, ALU.mult).then_inc(empty, 1)
                        e.tensor_reduce(now[:], sel.rearrange("p t c -> p c t"), AX.X, ALU.add)
                        e.drain()
                        e.tensor_tensor(taken[:], taken[:], now[:], ALU.add).then_inc(weighed.sem, 1)
                    elif kind == "u":
                        j = step[1]
                        n = P if j < NP else I
                        e.wait_ge(*silued_of(ring, b, j))
                        e.wait_ge(*ring.written(b, step))
                        if j < NP:
                            e.tensor_tensor(hh[:, j % 2], bank[:], sil[:, j % 2], ALU.mult).then_inc(empty, 1)
                        else:
                            e.wait_ge(*down(b, j, 2))
                            e.tensor_tensor(h2[0:n, j % 2], bank[0:n], sil[0:n, j % 2], ALU.mult).then_inc(empty, 1)
                            e.drain().then_inc(h_ready.sem, 1)
                    elif kind == "w":
                        j = step[1]
                        e.drain()
                        e.wait_ge(*ring.written(b, step))
                        e.wait_ge(*down(b, j, 2))
                        e.tensor_tensor(h2[:, j % 2], bank[:], hh[:, j % 2], ALU.mult).then_inc(empty, 1)
                        e.drain().then_inc(h_ready.sem, 1)
                e.wait_ge(*fb_ready(b, "fb"))
                e.wait_ge(*down(b, NP))
                e.tensor_copy(g.f[:, bass.ds(b * TT, TT), :], acc.rearrange("p (t c) -> p t c", t=TT)).then_inc(stored.sem, 1)

        @block.tensor
        def _(e):
            e.wait_ge(loaded, N_DMA)

            def add(b, j):
                n = P if j < NP else I
                e.wait_ge(*h_ready(b, j))
                if j == 0:
                    e.wait_ge(*stored(b, "f", 1))
                rhs = wd[:, j, :] if j < NP else sd[:]
                for tt in range(TT):
                    o = e.matmul(acc[:, tt * C:tt * C + C], h2[0:n, j % 2, tt * P:tt * P + P], rhs,
                                 start=(j == 0 and tt == 0), stop=(j == NP), skip_group_check=True)
                o.then_inc(down.sem, 1)

            with e.Fori(0, BATCH) as b:
                for step in RING:
                    kind = step[0]
                    bank, full = ring.at(step), ring.full_of(step)
                    if kind == "turn":
                        e.wait_ge(*ring.free(b, step))
                        e.wait_ge(*fb_ready(b, "fb"))
                        for tt in range(TT):
                            o = e.transpose(bank[:, tt * P:tt * P + P], fb[:, tt], g.ident[:])
                    elif kind == "logits":
                        e.wait_ge(*ring.free(b, step))
                        e.wait_ge(*ring.read(b, ("turn",)))
                        for tt in range(TT):
                            o = e.matmul(bank[:, tt * E:tt * E + E], xT[:, tt * P:tt * P + P], router[:], start=True, stop=True)
                    elif kind == "pos":
                        e.wait_ge(*ring.free(b, step))
                        e.wait_ge(*chosen(b, "sel"))
                        e.wait_ge(*weighed(b, "w", 1))
                        for tt in range(TT):
                            out = bank[:, tt * E:tt * E + E]
                            e.matmul(out, g.ones[:], taken[:], start=True, stop=False)
                            for t in range(tt):
                                e.matmul(out, g.ones[:], sel[:, t], start=False, stop=False)
                            o = e.matmul(out, g.before[:], sel[:, tt], start=False, stop=True)
                    elif kind == "wturn":
                        e.wait_ge(*ring.free(b, step))
                        e.wait_ge(*weighed(b, "w"))
                        e.sem_inc(passed, 1)
                        for tt in range(TT):
                            o = e.transpose(bank[0:E, tt * P:tt * P + P], wt[:, tt], g.ident[:])
                    else:
                        j = step[1]
                        e.wait_ge(*ring.free(b, step))
                        if kind == "w":
                            if j == 0:
                                e.wait_ge(*ring.read(b, ("wturn",)))
                            o = e.matmul(bank[:], pick[:, 2 * j:2 * j + 2, :], wT[:], start=True, stop=True)
                        else:
                            lhs = {"g": (wg, sg), "u": (wu, su)}[kind]
                            lhs, n = (lhs[0][:, j, :], P) if j < NP else (lhs[1][:], I)
                            o = e.matmul(bank[0:n], lhs, xT[:], start=True, stop=True)
                    o.then_inc(full, 1)
                    if kind == "u" and step[1]:
                        add(b, step[1] - 1)
                add(b, NP)


def silued_of(ring, b, j):
    return ring.read(b, ("g", j))


def quat_net(nc, g, name, w):
    NQ = C // 4
    TERMS = [[(1, 0, 0), (-1, 1, 1), (-1, 2, 2), (-1, 3, 3)],
             [(1, 0, 1), (1, 1, 0), (1, 2, 3), (-1, 3, 2)],
             [(1, 0, 2), (-1, 1, 3), (1, 2, 0), (1, 3, 1)],
             [(1, 0, 3), (1, 1, 2), (-1, 2, 1), (1, 3, 0)]]

    def comp(t, c):
        return t[:, :, c * NQ:(c + 1) * NQ]

    def quaternion_product(e, out, a, b, tmp, conj):
        n = 0
        for c, terms in enumerate(TERMS):
            for k, (sign, x, y) in enumerate(terms):
                if conj and y:
                    sign = -sign
                if k == 0:
                    e.scalar_tensor_tensor(comp(out, c), comp(a, x), float(sign), comp(b, y), ALU.mult, ALU.mult)
                    continue
                t = tmp[:, n % 2]
                n += 1
                e.tensor_tensor(t, comp(a, x), comp(b, y), ALU.mult)
                e.drain()
                e.tensor_tensor(comp(out, c), comp(out, c), t, ALU.add if sign > 0 else ALU.subtract)
        e.drain()

    with ExitStack() as shared:
        sb = lambda n, shape: shared.enter_context(nc.sbuf_tensor(f"{name}_{n}", shape, F32))
        keys = sb("keys", [P, NT, C])
        vals = sb("vals", [P, NT, C])
        bound = sb("bound", [P, NT, C])
        tmp = sb("tmp", [P, 2, NT, NQ])
        wk = sb("wk", [P, C])
        wv = sb("wv", [P, C])
        wo = sb("wo", [P, C])
        rows = sb("rows", [P, 3, C])
        ln = sb("ln", [P, 2])
        isq = sb("isq", [P, TT])
        LOADED = 16 * 6

        with stage(nc, name + "k") as r:
            fb = r.sb("fb", [P, TT, C])
            xT = r.sb("xT", [P, SEQ])
            ksq = r.sb("ksq", [P, TT, C])
            nsq = r.sb("nsq", [P, TT, NQ])
            kb = r.sb("kb", [P, TT, C])
            ring = r.banks("ring", [r.ps(f"ring{i}", [P, 512]) for i in range(3)], ["turn", "k", "v"])
            loaded, passed, halved = r.sem("loaded"), r.sem("passed"), r.sem("halved")
            fb_ready = r.count("fb_ready", ["f"])
            squared = r.count("squared", ["s"])
            normed = r.count("normed", ["n"])
            scaled = r.count("scaled", ["k"])
            block = r.block()

            @block.sync
            def _(e):
                r.give_credit(e)
                for dst, src in ((wk, "wk"), (wv, "wv"), (wo, "wo"), (ln, "ln"), (isq, "isq")):
                    e.dma_start(dst[:], w[src]).then_inc(loaded, 16)
                e.dma_start(rows.rearrange("p a b -> p (a b)"), w["rows"].broadcast_to([P, 3 * C])).then_inc(loaded, 16)
                e.wait_ge(loaded, LOADED)

            @block.gpsimd
            def _(e):
                with e.Fori(0, BATCH) as b:
                    e.wait_ge(*ring.written(b, "turn", 1))
                    e.sem_inc(passed, 1)
                    e.tensor_copy(fb[:], g.f[:, bass.ds(b * TT, TT), :]).then_inc(fb_ready.sem, 1)

            @block.tensor
            def _(e):
                e.wait_ge(loaded, LOADED)
                with e.Fori(0, BATCH) as b:
                    for what in ("turn", "k", "v"):
                        bank = ring.at(what)
                        e.wait_ge(*ring.free(b, what))
                        e.wait_ge(*(fb_ready(b, "f") if what == "turn" else ring.read(b, "turn")))
                        for tt in range(TT):
                            out = bank[:, tt * P:tt * P + P]
                            if what == "turn":
                                o = e.transpose(out, fb[:, tt], g.ident[:])
                            else:
                                o = e.matmul(out, xT[:, tt * P:tt * P + P], (wk if what == "k" else wv)[:], start=True, stop=True)
                        o.then_inc(ring.full_of(what), 1)

            @block.scalar
            def _(e):
                with e.Fori(0, BATCH) as b:
                    e.wait_ge(*ring.written(b, "v", 1))
                    e.wait_ge(*ring.written(b, "turn"))
                    e.activation(xT[:], ring.at("turn")[:], ACT.Copy).then_inc(ring.empty_of("turn"), 1)
                    e.wait_ge(*squared(b, "s"))
                    e.activation(nsq[:], nsq[:], ACT.Sqrt).then_inc(normed.sem, 1)

            @block.vector
            def _(e):
                e.wait_ge(loaded, LOADED)
                tiles = lambda t: t.rearrange("p (t c) -> p t c", t=TT)
                with e.Fori(0, BATCH) as b:
                    here = bass.ds(b * TT, TT)
                    e.wait_ge(*ring.written(b, "k"))
                    e.tensor_tensor(kb[:], tiles(ring.at("k")), spread(rows[:, 0], 1, TT), ALU.add).then_inc(ring.empty_of("k"), 1)
                    e.drain()
                    e.tensor_tensor(ksq[:], kb[:], kb[:], ALU.mult)
                    e.drain()
                    e.tensor_reduce(nsq[:], ksq.rearrange("p t (q i) -> p t i q", q=4), AX.X, ALU.add)
                    e.drain()
                    e.tensor_scalar(nsq[:], nsq[:], 1e-24, None, ALU.max)
                    e.drain().then_inc(squared.sem, 1)
                    e.wait_ge(*ring.written(b, "v"))
                    e.tensor_tensor(vals[:, here], tiles(ring.at("v")), spread(rows[:, 1], 1, TT), ALU.add).then_inc(ring.empty_of("v"), 1)
                    e.wait_ge(*normed(b, "n"))
                    e.reciprocal(nsq[:], nsq[:])
                    e.drain()
                    for q in range(4):
                        e.tensor_tensor(keys[:, here, q * NQ:(q + 1) * NQ], kb[:, :, q * NQ:(q + 1) * NQ], nsq[:], ALU.mult)
                    e.drain()
                quaternion_product(e, bound, vals, keys, tmp, False)

        with stage(nc, name + "c") as r:
            m_ps = [r.ps(f"m{i}", [P, 512]) for i in range(2)]
            cumulated = [r.count(f"cumulated{i}", ["m"]) for i in range(2)]
            copied = [r.count(f"copied{i}", ["m"]) for i in range(2)]
            block = r.block()

            @block.sync
            def _(e):
                r.give_credit(e)

            @block.tensor
            def _(e):
                with e.Fori(0, BATCH // 2) as b2:
                    for s in range(2):
                        e.wait_ge(*copied[s](b2, "m", 1))
                        tile = lambda tt: bound[:, bass.ds(b2 * (2 * TT) + (s * TT + tt), 1), :]
                        for tt in range(TT):
                            out = m_ps[s][:, tt * P:tt * P + P]
                            for t in range(tt):
                                e.matmul(out, g.ones[:], tile(t), start=t == 0, stop=False)
                            o = e.matmul(out, g.upto[:], tile(tt), start=tt == 0, stop=True)
                        o.then_inc(cumulated[s].sem, 1)

            @block.scalar
            def _(e):
                with e.Fori(0, BATCH // 2) as b2:
                    for s in range(2):
                        e.wait_ge(*cumulated[s](b2, "m"))
                        e.activation(vals[:, bass.ds(b2 * (2 * TT) + s * TT, TT), :],
                                     m_ps[s].rearrange("p (t c) -> p t c", t=TT), ACT.Copy).then_inc(copied[s].sem, 1)

            @block.vector
            def _(e):
                for s in range(2):
                    e.wait_ge(copied[s].sem, BATCH // 2 + 1)
                quaternion_product(e, bound, vals, keys, tmp, True)

        with stage(nc, name) as r:
            rb = r.sb("rb", [P, TT, C])
            stats = r.sb("stats", [P, TT, 6])
            mv = r.sb("mv", [P, TT, 2])
            rstd = r.sb("rstd", [P, TT])
            half = r.sb("half", [P, TT])
            eps = r.sb("eps", [P, TT])
            xn = r.sb("xn", [P, TT, C])
            nT = r.sb("nT", [P, SEQ])
            y = r.sb("y", [P, TT, C])
            res = r.sb("res", [P, TT, C])
            ring = r.banks("ring", [r.ps(f"ring{i}", [P, 512]) for i in range(2)], ["turn", "out"])
            passed = r.sem("passed")
            measured = r.count("measured", ["m"])
            rstd_ready = r.count("rstd_ready", ["r"])
            normed = r.count("normed", ["n"])
            res_ready = r.count("res_ready", ["s"])
            sent = r.sem("sent")
            block = r.block()

            @block.sync
            def _(e):
                r.give_credit(e)
                e.sem_inc(sent, 16)
                with e.Fori(0, BATCH) as b:
                    e.wait_ge(*res_ready(b, "s"))
                    e.dma_start(g.s_dram[bass.ds(b, 1)].rearrange("o (t p) c -> p (o t) c", p=P), res[:]).then_inc(sent, 16)
                e.wait_ge(sent, 16 * (BATCH + 1))

            @block.gpsimd
            def _(e):
                e.memset(half[:], -0.5)
                e.memset(eps[:], EPS)
                e.drain()
                with e.Fori(0, BATCH) as b:
                    e.wait_ge(*measured(b, "m"))
                    e.tensor_tensor(rstd[:], mv[:, :, 1], eps[:], ALU.add)
                    e.drain()
                    e.tensor_tensor(rstd[:], rstd[:], half[:], ALU.pow).then_inc(rstd_ready.sem, 1)

            @block.vector
            def _(e):
                with e.Fori(0, BATCH) as b:
                    here = bass.ds(b * TT, TT)
                    e.tensor_tensor(rb[:], bound[:, here], spread(isq[:], 2, C), ALU.mult)
                    e.drain()
                    for tt in range(TT):
                        e.bn_stats(stats[:, tt], rb[:, tt])
                    e.drain()
                    for tt in range(TT):
                        e.bn_aggr(mv[:, tt], stats[:, tt])
                    e.drain().then_inc(measured.sem, 1)
                    e.wait_ge(*rstd_ready(b, "r"))
                    e.wait_ge(*ring.written(b, "turn", 1))
                    for tt in range(TT):
                        o = e.tensor_scalar(xn[:, tt], rb[:, tt], mv[:, tt, 0:1], rstd[:, tt:tt + 1], ALU.subtract, ALU.mult)
                    o.then_inc(normed.sem, 1)
                    e.wait_ge(*ring.written(b, "out"))
                    e.tensor_tensor(y[:], ring.at("out").rearrange("p (t c) -> p t c", t=TT), spread(rows[:, 2], 1, TT),
                                    ALU.add).then_inc(ring.empty_of("out"), 1)
                    e.drain()
                    e.wait_ge(sent, b * 16 + 16)
                    e.tensor_tensor(res[:], y[:], g.f[:, here], ALU.add).then_inc(res_ready.sem, 1)
                    e.drain()

            @block.scalar
            def _(e):
                with e.Fori(0, BATCH) as b:
                    e.wait_ge(*ring.written(b, "out", 1))
                    e.wait_ge(*ring.written(b, "turn"))
                    e.activation(nT[:], ring.at("turn")[:], ACT.Identity, bias=ln[:, 1:2],
                                 scale=ln[:, 0:1]).then_inc(ring.empty_of("turn"), 1)

            @block.tensor
            def _(e):
                with e.Fori(0, BATCH) as b:
                    for what in ("turn", "out"):
                        bank = ring.at(what)
                        e.wait_ge(*ring.free(b, what))
                        e.wait_ge(*(normed(b, "n") if what == "turn" else ring.read(b, "turn")))
                        for tt in range(TT):
                            out = bank[:, tt * P:tt * P + P]
                            if what == "turn":
                                o = e.transpose(out, xn[:, tt], g.ident[:])
                            else:
                                o = e.matmul(out, nT[:, tt * P:tt * P + P], wo[:], start=True, stop=True)
                        o.then_inc(ring.full_of(what), 1)


def route_net(nc, g, name, w):
    E, NGRP, F = 8, 4, 341
    KTOK = BATCH * SEQ // E
    chunks = [(o, min(P, F - o)) for o in range(0, F, P)]
    NC = len(chunks)
    with ExitStack() as shared:
        sb = lambda n, shape, dt=F32: shared.enter_context(nc.sbuf_tensor(f"{name}_{n}", shape, dt))
        xT = sb("xT", [P, BATCH, SEQ])
        rate = sb("rate", [P, NT, E])
        wr = sb("wr", [P, E])
        br = sb("br", [P, E])
        wu = sb("wu", [P, NGRP, F])
        bu = sb("bu", [P, NGRP, NC])
        wd = sb("wd", [P, NC, NGRP, 2 * C])
        bd = sb("bd", [E, C])

        with stage(nc, name + "s") as r:
            fb = r.sb("fb", [P, 2, TT, C])
            fbT = r.sb("fbT", [P, SEQ])
            lg = r.sb("lg", [P, TT, E])
            mx = r.sb("mx", [P, TT])
            ex = r.sb("ex", [P, TT, E])
            sm = r.sb("sm", [P, TT])
            t_ps = r.ps("t", [P, 512])
            l_ps = r.ps("l", [P, 512])
            loaded, passed = r.sem("loaded"), r.sem("passed")
            fb_ready = r.count("fb_ready", ["f"])
            turned = r.count("turned", ["t"])
            copied = r.count("copied", ["x"])
            rated = r.count("rated", ["l"])
            shifted = r.count("shifted", ["s"])
            exped = r.count("exped", ["e"])
            block = r.block()

            @block.sync
            def _(e):
                r.give_credit(e)
                e.dma_start(wr[:], w["wr"]).then_inc(loaded, 16)
                e.dma_start(br[:], w["br"].broadcast_to([P, E])).then_inc(loaded, 16)
                for dst, src in ((wu, "wu"), (bu, "bu"), (wd, "wd"), (bd, "bd")):
                    e.dma_start(dst[:], w[src]).then_inc(loaded, 16)
                e.wait_ge(loaded, 96)

            @block.gpsimd
            def _(e):
                with e.Fori(0, BATCH) as b:
                    e.wait_ge(*turned(b, "t", 1))
                    e.sem_inc(passed, 1)
                    e.tensor_copy(fb[:, 0], g.f[:, bass.ds(b * TT, TT), :]).then_inc(fb_ready.sem, 1)

            @block.tensor
            def _(e):
                e.wait_ge(loaded, 96)
                with e.Fori(0, BATCH) as b:
                    e.wait_ge(*fb_ready(b, "f"))
                    e.wait_ge(*copied(b, "x", 1))
                    for tt in range(TT):
                        o = e.transpose(t_ps[:, tt * P:tt * P + P], fb[:, 0, tt], g.ident[:])
                    o.then_inc(turned.sem, 1)
                    e.wait_ge(*copied(b, "x"))
                    e.wait_ge(*shifted(b, "s", 1))
                    for tt in range(TT):
                        o = e.matmul(l_ps[:, tt * E:tt * E + E], fbT[:, tt * P:tt * P + P], wr[:], start=True, stop=True)
                    o.then_inc(rated.sem, 1)

            @block.scalar
            def _(e):
                with e.Fori(0, BATCH) as b:
                    e.wait_ge(*turned(b, "t"))
                    e.wait_ge(*rated(b, "l", 1))
                    e.activation(fbT[:], t_ps[:], ACT.Copy)
                    e.activation(xT[:, bass.ds(b, 1), :].rearrange("p o c -> p (o c)"), t_ps[:], ACT.Copy).then_inc(copied.sem, 1)
                    e.wait_ge(*shifted(b, "s"))
                    e.activation(ex[:], lg[:], ACT.Exp).then_inc(exped.sem, 1)

            @block.vector
            def _(e):
                e.wait_ge(loaded, 96)
                with e.Fori(0, BATCH) as b:
                    e.wait_ge(*rated(b, "l"))
                    e.tensor_tensor(lg[:], l_ps[:, 0:TT * E].rearrange("p (t e) -> p t e", t=TT), spread(br[:], 1, TT), ALU.add)
                    e.drain()
                    e.tensor_reduce(mx[:], lg[:], AX.X, ALU.max)
                    e.drain()
                    e.tensor_tensor(lg[:], lg[:], spread(mx[:], 2, E), ALU.subtract)
                    e.drain().then_inc(shifted.sem, 1)
                    e.wait_ge(*exped(b, "e"))
                    e.tensor_reduce(sm[:], ex[:], AX.X, ALU.add)
                    e.drain()
                    e.reciprocal(sm[:], sm[:])
                    e.drain()
                    e.tensor_tensor(rate[:, bass.ds(b * TT, TT), :], ex[:], spread(sm[:], 2, E), ALU.mult)
                    e.drain()

        with stage(nc, name + "b") as r:
            kth = r.sb("kth", [P, E], I32)
            cand = r.sb("cand", [P, E], I32)
            bit = r.sb("bit", [P, E], I32)
            add = r.sb("add", [P, E], I32)
            hit = r.sb("hit", [P, NT, E])
            cnt = r.sb("cnt", [P, E])
            eq = r.sb("eq", [P, NT, E])
            room_left = r.sb("room_left", [P, E])
            before = r.sb("before", [P, E, NT])
            one = r.sb("one", [P, NT])
            n_ps = r.ps("n", [P, E])
            e_ps = r.ps("equal_before", [P, NT, E])
            i_ps = r.ps("equal_in", [P, NT, E])
            counted = r.count("counted", ["c"])
            summed = r.count("summed", ["s"])
            greater, greater_sum, equal, equal_sum = (r.sem(n) for n in ("greater", "greater_sum", "equal", "equal_sum"))
            BITS = 30
            block = r.block()

            @block.sync
            def _(e):
                r.give_credit(e)

            @block.vector
            def _(e):
                e.memset(kth[:], 0)
                e.memset(bit[:], 1 << (BITS - 1))
                e.memset(one[:], 1.0)
                e.drain()
                with e.Fori(0, BITS) as i:
                    e.tensor_tensor(cand[:], kth[:], bit[:], ALU.bitwise_or)
                    e.drain()
                    e.tensor_tensor(hit[:], rate[:], spread(cand.bitcast(F32)[:], 1, NT), ALU.is_ge)
                    e.drain()
                    e.tensor_reduce(cnt[:], hit.rearrange("p t e -> p e t"), AX.X, ALU.add).then_inc(counted.sem, 1)
                    e.wait_ge(*summed(i, "s"))
                    e.tensor_scalar(cnt[:], n_ps[:], KTOK - 0.5, None, ALU.is_ge)
                    e.drain()
                    e.tensor_tensor(add[:], cnt[:], bit[:], ALU.mult)
                    e.drain()
                    e.tensor_tensor(kth[:], kth[:], add[:], ALU.bitwise_or)
                    e.tensor_scalar(bit[:], bit[:], 1, None, ALU.logical_shift_right)
                    e.drain()
                value = kth.bitcast(F32)[:]
                e.tensor_tensor(hit[:], rate[:], spread(value, 1, NT), ALU.is_gt)
                e.tensor_tensor(eq[:], rate[:], spread(value, 1, NT), ALU.is_equal)
                e.drain()
                e.tensor_reduce(cnt[:], hit.rearrange("p t e -> p e t"), AX.X, ALU.add)
                e.drain().then_inc(greater, 1)
                e.wait_ge(greater_sum, 1)
                e.tensor_scalar(room_left[:], n_ps[:], -1.0, float(KTOK), ALU.mult, ALU.add)
                for x in range(E):
                    e.tensor_tensor_scan(before[:, x], one[:], i_ps[:, :, x], 0.0, ALU.mult, ALU.add)
                e.drain()
                e.tensor_tensor(before[:], before[:], i_ps.rearrange("p t e -> p e t"), ALU.subtract)
                e.drain()
                e.tensor_tensor(before[:], before[:], e_ps.rearrange("p t e -> p e t"), ALU.add)
                e.drain()
                for x in range(E):
                    e.tensor_scalar(before[:, x], before[:, x], room_left[:, x:x + 1], None, ALU.is_lt)
                e.drain()
                e.tensor_tensor(eq[:], eq[:], before.rearrange("p e t -> p t e"), ALU.mult)
                e.drain()
                e.tensor_tensor(hit[:], hit[:], eq[:], ALU.add)
                e.drain()
                e.tensor_tensor(rate[:], rate[:], hit[:], ALU.mult)

            @block.tensor
            def _(e):
                with e.Fori(0, BITS) as i:
                    e.wait_ge(*counted(i, "c"))
                    e.matmul(n_ps[:], g.ones[:], cnt[:], start=True, stop=True).then_inc(summed.sem, 1)
                e.wait_ge(greater, 1)
                e.matmul(n_ps[:], g.ones[:], cnt[:], start=True, stop=True)
                e.matmul(e_ps[:], g.before[:], eq[:], start=True, stop=True)
                e.matmul(i_ps[:], g.ones[:], eq[:], start=True, stop=True).then_inc(greater_sum, 1)

        UP = [("up", q, c) for q in range(NGRP) for c in range(NC)]
        DN = [("dn", q, t) for q in range(NGRP) for t in range(2)]
        USES = [("wt",), ("bias",)]
        for q in range(NGRP):
            USES += [("up", q, c) for c in range(NC)]
            if q:
                USES += [("dn", q - 1, t) for t in range(2)]
        USES += [("dn", NGRP - 1, t) for t in range(2)]
        NB = 8
        USES += [("spare", i) for i in range(-len(USES) % NB)]
        with stage(nc, name) as r:
            xb = r.sb("xb", [P, SEQ])
            rb = r.sb("rb", [P, TT, E])
            rT = r.sb("rT", [E, SEQ])
            mid = r.sb("mid", [P, 2, NC, SEQ])
            y = r.sb("y", [P, TT, C])
            ring = r.banks("ring", [r.ps(f"ring{i}", [P, 512]) for i in range(NB)], USES)
            passed = r.sem("passed")
            xb_ready = r.count("xb_ready", ["x"])
            y_ready = r.count("y_ready", ["y"])
            y_taken = r.count("y_taken", ["y"])
            block = r.block()

            @block.sync
            def _(e):
                r.give_credit(e)

            @block.gpsimd
            def _(e):
                with e.Fori(0, BATCH) as b:
                    e.wait_ge(*ring.written(b, ("up", NGRP - 1, NC - 1), 1))
                    e.wait_ge(*ring.written(b, ("wt",), 1))
                    e.wait_ge(*y_ready(b, "y", 1))
                    e.sem_inc(passed, 1)
                    e.tensor_copy(xb[:], xT[:, bass.ds(b, 1), :].rearrange("p o c -> p (o c)"))
                    e.tensor_copy(rb[:], rate[:, bass.ds(b * TT, TT), :])
                    e.drain().then_inc(xb_ready.sem, 1)
                    e.wait_ge(*y_ready(b, "y"))
                    e.sem_inc(passed, 1)
                    e.tensor_copy(g.f[:, bass.ds(b * TT, TT), :], y[:]).then_inc(y_taken.sem, 1)

            @block.tensor
            def _(e):
                with e.Fori(0, BATCH) as b:
                    for step in USES:
                        kind = step[0]
                        bank, full = ring.at(step), ring.full_of(step)
                        need = [ring.free(b, step)]
                        if kind == "wt":
                            need.append(xb_ready(b, "x"))
                        elif kind == "bias":
                            need.append(ring.read(b, ("wt",)))
                        elif kind == "dn":
                            need += [ring.read(b, ("up", step[1], c)) for c in range(NC)]
                        for n in furthest(*need):
                            e.wait_ge(*n)
                        if kind == "spare":
                            e.sem_inc(ring.full_of(step), 1)
                            e.sem_inc(ring.empty_of(step), 1)
                            continue
                        if kind == "wt":
                            for tt in range(TT):
                                o = e.transpose(bank[0:E, tt * P:tt * P + P], rb[:, tt], g.ident[:])
                        elif kind == "bias":
                            for tt in range(TT):
                                o = e.matmul(bank[:, tt * P:tt * P + P], rT[:, tt * P:tt * P + P], bd[:], start=True, stop=True)
                        elif kind == "up":
                            _, q, c = step
                            f0, n = chunks[c]
                            o = e.matmul(bank[0:n], wu[:, q, f0:f0 + n], xb[:], start=True, stop=True)
                        else:
                            _, q, t = step
                            for k in range(2):
                                tt = 2 * t + k
                                for c, (f0, n) in enumerate(chunks):
                                    o = e.matmul(bank[:, 256 * k:256 * k + 256], mid[0:n, q % 2, c, tt * P:tt * P + P],
                                                 wd[0:n, c, q, :], start=c == 0, stop=c == NC - 1)
                        o.then_inc(full, 1)

            @block.scalar
            def _(e):
                with e.Fori(0, BATCH) as b:
                    for step in USES:
                        kind = step[0]
                        if kind == "wt":
                            need = [ring.written(b, step), ring.written(b, ("bias",), 1)]
                        elif kind == "up":
                            _, q, c = step
                            need = [ring.written(b, step)]
                            if q >= 2:
                                need.append(ring.written(b, ("dn", q - 2, 1)))
                            else:
                                need.append(ring.written(b, ("dn", NGRP - 2 + q, 1), 1))
                        else:
                            continue
                        for n in furthest(*need):
                            e.wait_ge(*n)
                        bank, empty = ring.at(step), ring.empty_of(step)
                        if kind == "wt":
                            e.activation(rT[:], bank[0:E], ACT.Copy).then_inc(empty, 1)
                        else:
                            n = chunks[c][1]
                            e.activation(mid[0:n, q % 2, c], bank[0:n], ACT.Silu, bias=bu[0:n, q, c:c + 1]).then_inc(empty, 1)

            @block.vector
            def _(e):
                with e.Fori(0, BATCH) as b:
                    for step in USES:
                        kind = step[0]
                        bank, empty = ring.at(step), ring.empty_of(step)
                        if kind == "bias":
                            e.wait_ge(*y_taken(b, "y", 1))
                            e.wait_ge(*ring.written(b, step))
                            e.tensor_copy(y[:], bank.rearrange("p (t c) -> p t c", t=TT)).then_inc(empty, 1)
                            e.drain()
                        elif kind == "dn":
                            _, q, t = step
                            e.wait_ge(*ring.written(b, step))
                            for x in range(2):
                                for k in range(2):
                                    tt = 2 * t + k
                                    col = 256 * k + x * C
                                    ex_ = 2 * q + x
                                    o = e.scalar_tensor_tensor(y[:, tt], bank[:, col:col + C], rb[:, tt, ex_:ex_ + 1], y[:, tt],
                                                               ALU.mult, ALU.add)
                                if x:
                                    o.then_inc(empty, 1)
                                e.drain()
                    e.drain().then_inc(y_ready.sem, 1)


def combine(nc, g, name, x_in, x_out, mixed, again):
    with stage(nc, name) as r:
        xb = r.sb("xb", [P, 2, TT, C])
        sb_ = r.sb("s", [P, 2, TT, C])
        fb = r.sb("fb", [P, 2, TT, C])
        xo = r.sb("xo", [P, 2, TT, C])
        stats = r.sb("stats", [P, TT, 6])
        mv = r.sb("mv", [P, TT, 2])
        rstd = r.sb("rstd", [P, TT])
        half = r.sb("half", [P, TT])
        eps = r.sb("eps", [P, TT])
        loaded = [r.sem(f"loaded{k}") for k in range(2)]
        sent = [r.sem(f"sent{k}") for k in range(2)]
        silued = r.count("silued", [0, 1])
        added = r.count("added", [0, 1])
        measured = r.count("measured", [0, 1])
        rstd_ready = r.count("rstd_ready", [0, 1])
        block = r.block()
        PER = 32 if mixed else 16

        def pairs(e, body):
            with e.Fori(0, BATCH // 2) as h:
                for k in range(2):
                    body(h, k, h * 2 + k)

        @block.sync
        def _(e):
            r.give_credit(e)
            view = lambda t, b: t[bass.ds(b, 1)].rearrange("o (t p) c -> p (o t) c", p=P)

            def load(h, k, b):
                e.wait_ge(*added(h, k, 2))
                e.dma_start(xb[:, k], view(x_in, b)).then_inc(loaded[k], 16)
                if mixed:
                    e.dma_start(sb_[:, k], view(g.s_dram, b)).then_inc(loaded[k], 16)
            pairs(e, load)

        @block.scalar
        def _(e):
            view = lambda t, b: t[bass.ds(b, 1)].rearrange("o (t p) c -> p (o t) c", p=P)
            for k in range(2):
                e.sem_inc(sent[k], 16)

            def body(h, k, b):
                if mixed:
                    e.wait_ge(*added(h, k, 2))
                    e.activation(fb[:, k], g.f[:, bass.ds(b * TT, TT), :], ACT.Silu).then_inc(silued.sem, 1)
                if x_out is not None:
                    e.wait_ge(*added(h, k))
                    e.dma_start(view(x_out, b), xo[:, k]).then_inc(sent[k], 16)
            if mixed or x_out is not None:
                pairs(e, body)
            if x_out is not None:
                for k in range(2):
                    e.wait_ge(sent[k], 16 * (BATCH // 2 + 1))

        @block.gpsimd
        def _(e):
            e.memset(half[:], -0.5)
            e.memset(eps[:], EPS)
            e.drain()

            def body(h, k, b):
                e.wait_ge(*measured(h, k))
                e.tensor_tensor(rstd[:], mv[:, :, 1], eps[:], ALU.add)
                e.drain()
                e.tensor_tensor(rstd[:], rstd[:], half[:], ALU.pow).then_inc(rstd_ready.sem, 1)
            if again:
                pairs(e, body)

        @block.vector
        def _(e):
            def body(h, k, b):
                e.wait_ge(loaded[k], h * PER + PER)
                if x_out is not None:
                    e.wait_ge(sent[k], h * 16 + 16)
                if mixed:
                    e.wait_ge(*silued(h, k))
                    e.tensor_tensor(sb_[:, k], sb_[:, k], fb[:, k], ALU.mult)
                    e.drain()
                    e.tensor_tensor(xo[:, k], sb_[:, k], xb[:, k], ALU.add)
                else:
                    e.tensor_copy(xo[:, k], xb[:, k])
                e.drain().then_inc(added.sem, 1)
                if not again:
                    return
                for tt in range(TT):
                    e.bn_stats(stats[:, tt], xo[:, k, tt])
                e.drain()
                for tt in range(TT):
                    e.bn_aggr(mv[:, tt], stats[:, tt])
                e.drain().then_inc(measured.sem, 1)
                e.wait_ge(*rstd_ready(h, k))
                for tt in range(TT):
                    e.tensor_scalar(g.f[:, bass.ds(b * TT + tt, 1), :].rearrange("p o c -> p (o c)"), xo[:, k, tt],
                                    mv[:, tt, 0:1], rstd[:, tt:tt + 1], ALU.subtract, ALU.mult)
                e.drain()
            pairs(e, body)


class Shared:
    pass


def build(nc, x, out, consts, nets):
    g = Shared()
    g.s_dram = nc.dram_tensor("mixer_out", (BATCH, SEQ, C), F32).ap()
    x_dram = nc.dram_tensor("residual", (BATCH, SEQ, C), F32).ap()
    with ExitStack() as ctx:
        g.f = ctx.enter_context(nc.sbuf_tensor("f", [P, NT, C], F32))
        const = {n: ctx.enter_context(nc.sbuf_tensor(f"const_{n}", [P, P], F32)) for n in consts}
        g.ident, g.down1, g.last1 = const["ident"], const["down1"], const["last1"]
        g.ones, g.before, g.upto = const["ones"], const["before"], const["upto"]
        g.ident_bf = ctx.enter_context(nc.sbuf_tensor("ident_bf", [P, P], BF16))
        with stage(nc, "consts") as r:
            loaded = r.sem("loaded")
            block = r.block()

            @block.sync
            def _(e):
                for n in consts:
                    e.dma_start(const[n][:], consts[n]).then_inc(loaded, 16)
                e.wait_ge(loaded, 16 * len(consts))

            @block.vector
            def _(e):
                e.wait_ge(loaded, 16 * len(consts))
                e.tensor_copy(g.ident_bf[:], g.ident[:])

        combine(nc, g, "n0", x, None, False, True)
        mamba_net(nc, g, "L0a", nets["L0_attn"], center=False, residual=False)
        local_attention_net(nc, g, "L0f", 16, 32, 6, nets["L0_ffn"])
        combine(nc, g, "n1", x, x_dram, True, True)
        ttt_net(nc, g, "L1a", nets["L1_attn"])
        local_attention_net(nc, g, "L1f", 8, 64, 2, nets["L1_ffn"])
        combine(nc, g, "n2", x_dram, x_dram, True, True)
        mamba_net(nc, g, "L2a", nets["L2_attn"], center=True, residual=True)
        moe_net(nc, g, "L2f", nets["L2_ffn"])
        combine(nc, g, "n3", x_dram, x_dram, True, True)
        quat_net(nc, g, "L3a", nets["L3_attn"])
        route_net(nc, g, "L3f", nets["L3_ffn"])
        combine(nc, g, "n4", x_dram, out, True, False)


def kernel(**inputs):
    import concourse.bacc as bacc
    from concourse.bass_utils import run_bass_kernel_spmd

    nc = bacc.Bacc("TRN2", target_bir_lowering=False, num_devices=1)
    arrays = {}

    def dram(name, a):
        a = np.ascontiguousarray(a)
        arrays[name] = a
        return nc.dram_tensor(name, a.shape, mybir.dt.from_np(a.dtype), kind="ExternalInput").ap()

    laid_out = {
        "L0_attn": lay_out_mamba(inputs, "L0_attn", MAMBA_NAMES["L0_attn"]),
        "L0_ffn": lay_out_attention(inputs, "L0_ffn", ATTENTION_NAMES["L0_ffn"]),
        "L1_attn": lay_out_ttt(inputs),
        "L1_ffn": lay_out_attention(inputs, "L1_ffn", ATTENTION_NAMES["L1_ffn"]),
        "L2_attn": lay_out_mamba(inputs, "L2_attn", MAMBA_NAMES["L2_attn"]),
        "L2_ffn": lay_out_moe(inputs),
        "L3_attn": lay_out_quat(inputs),
        "L3_ffn": lay_out_route(inputs),
    }
    for net, window in (("L0_ffn", 32), ("L1_ffn", 64)):
        laid_out[net]["rope"] = rotary_constants(window)
        laid_out[net]["mask"] = window_mask(window)
    nets = {net: {k: dram(f"{net}_{k}_dram", a) for k, a in ws.items()} for net, ws in laid_out.items()}
    consts = {k: dram(f"const_{k}_dram", a) for k, a in shape_constants().items()}
    x = dram("x_dram", np.asarray(inputs["L0_attn_x"]))
    out = nc.dram_tensor("out_dram", (BATCH, SEQ, C), F32, kind="ExternalOutput").ap()
    build(nc, x, out, consts, nets)
    r = run_bass_kernel_spmd(nc, [arrays], core_ids=[0])
    return r.results[0]["out_dram"]
```
